# Optimizing a Trainium2 kernel written in Bass

```python
import numpy as np
import jax
import jax.numpy as jnp

def _softmax(x, axis=-1):
    return jax.nn.softmax(x, axis=axis)

def _gelu(x):
    return jax.nn.gelu(x, approximate=True)

def _silu(x):
    return jax.nn.silu(x)

def _sigmoid(x):
    return jax.nn.sigmoid(x)

def _layernorm(x, axis=-1, eps=1e-05):
    m = jnp.mean(x, axis=axis, keepdims=True)
    v = jnp.var(x, axis=axis, keepdims=True)
    return (x - m) / jnp.sqrt(v + eps)

def _scatter_add(tgt, idx, src, axis=0):
    return tgt.at[idx].add(src)

def _segment_sum(src, seg, n):
    return jax.ops.segment_sum(src, seg, n)
kernel_name = 'mk_decoder_postln_d2_seqx_r8_bd1dc7'

def setup_inputs(seed: int=0):
    np.random.seed(seed)
    _w = jnp.asarray

    def _rec_inputs():
        import jax
        import jax.numpy as jnp
        _rk = jax.random.key(seed)
        x = -0.0002928 + 1 * jax.random.normal(jax.random.fold_in(_rk, 1), (4, 256, 128), jnp.float32)
        _lenS = 256 - jax.random.randint(jax.random.fold_in(_rk, 7), (4,), 0, max(1, 256 // 4) + 1, jnp.int32)
        _lenS2 = 256 - jax.random.randint(jax.random.fold_in(_rk, 8), (4,), 0, max(1, 256 // 4) + 1, jnp.int32)
        _ctx_1024P = jax.random.normal(jax.random.fold_in(_rk, 11), (4, 16, 128), jnp.float32)
        _ctx_1024c = jax.random.dirichlet(jax.random.fold_in(_rk, 511), 0.3 * jnp.ones((16,), jnp.float32), (4, 256))
        _ctx_1024t = jnp.einsum('bsk,bkd->bsd', _ctx_1024c, _ctx_1024P)
        _ctx_1024t = _ctx_1024t * jax.lax.rsqrt(jnp.mean(jnp.square(_ctx_1024t)) + 1e-12) * 0.953939
        ctx_1024 = -1.39393e-06 + 0.999914 * (_ctx_1024t + 0.3 * jax.random.normal(jax.random.fold_in(_rk, 611), (4, 256, 128), jnp.float32))
        _validS = jnp.arange(256)[None, :] < _lenS[:, None]
        _validS2 = jnp.arange(256)[None, :] < _lenS2[:, None]
        _causal = jnp.tril(jnp.ones((256, 256), dtype=bool))
        mask_Bx1x1xS2_if1 = jnp.where(jnp.ones((4, 1, 1, 256), dtype=bool), 1, 0).astype(jnp.int32)
        mask_1x1xSxS2_ik0 = jnp.where(jnp.broadcast_to(_validS2[0:1, None, None, :], (1, 1, 256, 256)), 0, 1).astype(jnp.int32)
        return (x, ctx_1024, mask_Bx1x1xS2_if1, mask_1x1xSxS2_ik0)
    x, ctx_1024, mask_Bx1x1xS2_if1, mask_1x1xSxS2_ik0 = _rec_inputs()

    def _L0_attn_setup():
        import jax, jax.numpy as jnp
        import numpy as np
        NUM_HEADS = 16
        key = jax.random.key(seed)
        ks = jax.random.split(key, 6)
        b, s, d = (2, 256, 128)
        scale = 1.0 / np.sqrt(d)
        return {'x': jax.random.normal(ks[0], (b, s, d), dtype=jnp.float32), 'Wq': jax.random.normal(ks[1], (d, d), dtype=jnp.float32) * scale, 'Wk': jax.random.normal(ks[2], (d, d), dtype=jnp.float32) * scale, 'Wv': jax.random.normal(ks[3], (d, d), dtype=jnp.float32) * scale, 'Wo': jax.random.normal(ks[4], (d, d), dtype=jnp.float32) * scale, 'bo': jnp.zeros((d,), dtype=jnp.float32)}
    _L0_attn_all = _L0_attn_setup()
    _L0_attn_in = {k: v for k, v in _L0_attn_all.items() if k in ('Wq', 'Wk', 'Wv', 'Wo', 'bo')}
    del _L0_attn_all

    def _L0_xattn_setup():
        import jax, jax.numpy as jnp
        import numpy as np
        import math
        D, NH, DFF = (128, 16, 512)
        B, S = (2, 256)
        EPS = 1e-05

        def _mha(q_in, k_in, v_in, wq, bq, wk, bk, wv, bv, wo, bo, mask):
            Bq, Sq, Dm = q_in.shape
            Sk = k_in.shape[1]
            dh = Dm // NH
            q = (q_in @ wq + bq).reshape(Bq, Sq, NH, dh).transpose(0, 2, 1, 3)
            k = (k_in @ wk + bk).reshape(Bq, Sk, NH, dh).transpose(0, 2, 1, 3)
            v = (v_in @ wv + bv).reshape(Bq, Sk, NH, dh).transpose(0, 2, 1, 3)
            scores = jnp.einsum('bhqd,bhkd->bhqk', q, k) / math.sqrt(dh)
            scores = jnp.where(mask == 0, jnp.float32(-1000000000.0), scores)
            w = jax.nn.softmax(scores, axis=-1)
            out = jnp.einsum('bhqk,bhkd->bhqd', w, v)
            out = out.transpose(0, 2, 1, 3).reshape(Bq, Sq, Dm)
            return out @ wo + bo

        def _ln(x, g, b):
            mu = jnp.mean(x, axis=-1, keepdims=True)
            var = jnp.var(x, axis=-1, keepdims=True)
            return (x - mu) * jax.lax.rsqrt(var + EPS) * g + b
        key = jax.random.key(seed)
        ks = jax.random.split(key, 20)
        sc = 1.0 / math.sqrt(D)
        inp = {'x': jax.random.normal(ks[0], (B, S, D), jnp.float32), 'encoder_output': jax.random.normal(ks[1], (B, S, D), jnp.float32), 'src_mask': jnp.ones((B, 1, 1, S), jnp.int32), 'tgt_mask': jnp.tril(jnp.ones((S, S), jnp.int32))[None, None]}
        names = ['s_wq', 's_wk', 's_wv', 's_wo', 'c_wq', 'c_wk', 'c_wv', 'c_wo']
        for i, n in enumerate(names):
            inp[n] = jax.random.normal(ks[2 + i], (D, D), jnp.float32) * sc
            inp[n.replace('w', 'b')] = jnp.zeros((D,), jnp.float32)
        inp['ff_w1'] = jax.random.normal(ks[10], (D, DFF), jnp.float32) * sc
        inp['ff_b1'] = jnp.zeros((DFF,), jnp.float32)
        inp['ff_w2'] = jax.random.normal(ks[11], (DFF, D), jnp.float32) / math.sqrt(DFF)
        inp['ff_b2'] = jnp.zeros((D,), jnp.float32)
        for i in (1, 2, 3):
            inp[f'ln{i}_g'] = jnp.ones((D,), jnp.float32)
            inp[f'ln{i}_b'] = jnp.zeros((D,), jnp.float32)
        return inp
    _L0_xattn_all = _L0_xattn_setup()
    _L0_xattn_in = {k: v for k, v in _L0_xattn_all.items() if k in ('s_wq', 's_bq', 's_wk', 's_bk', 's_wv', 's_bv', 's_wo', 's_bo', 'c_wq', 'c_bq', 'c_wk', 'c_bk', 'c_wv', 'c_bv', 'c_wo', 'c_bo', 'ff_w1', 'ff_b1', 'ff_w2', 'ff_b2', 'ln1_g', 'ln1_b', 'ln2_g', 'ln2_b', 'ln3_g', 'ln3_b')}
    del _L0_xattn_all

    def _L0_ffn_setup():
        import jax, jax.numpy as jnp
        import numpy as np
        B, S, D = (2, 256, 128)
        E, G, K = (32, 8, 4)
        H, SH = (256, 256)
        CAP_FACTOR = 1.25

        def _l2norm(v):
            n = jnp.linalg.norm(v, axis=-1, keepdims=True)
            return v / jnp.maximum(n, 1e-12)
        key = jax.random.key(seed)
        ks = jax.random.split(key, 10)
        x = jax.random.normal(ks[0], (B, S, D), jnp.float32)
        group_centroids = jax.random.normal(ks[1], (G, D), jnp.float32) * 0.02
        expert_centroids = jax.random.normal(ks[2], (E, D), jnp.float32) * 0.02
        bias = jnp.zeros((E,), jnp.float32)
        sd_in = 1.0 / np.sqrt(D).astype(np.float32)
        sd_h = 1.0 / np.sqrt(H).astype(np.float32)
        wg = jax.random.normal(ks[3], (E, D, H), jnp.float32) * sd_in
        wu = jax.random.normal(ks[4], (E, D, H), jnp.float32) * sd_in
        wd = jax.random.normal(ks[5], (E, H, D), jnp.float32) * sd_h
        sg = jax.random.normal(ks[6], (D, SH), jnp.float32) * sd_in
        su = jax.random.normal(ks[7], (D, SH), jnp.float32) * sd_in
        sd_w = jax.random.normal(ks[8], (SH, D), jnp.float32) * sd_h
        return dict(x=x, group_centroids=group_centroids, expert_centroids=expert_centroids, bias=bias, wg=wg, wu=wu, wd=wd, sg=sg, su=su, sd=sd_w)
    _L0_ffn_all = _L0_ffn_setup()
    _L0_ffn_in = {k: v for k, v in _L0_ffn_all.items() if k in ('group_centroids', 'expert_centroids', 'bias', 'wg', 'wu', 'wd', 'sg', 'su', 'sd')}
    del _L0_ffn_all

    def _L1_attn_setup():
        import jax, jax.numpy as jnp
        import numpy as np
        B, S, E, H, W = (4, 256, 128, 16, 128)
        HD = E // H
        key = jax.random.key(seed)
        ks = jax.random.split(key, 5)
        scale = 1.0 / np.sqrt(E)
        x = jax.random.normal(ks[0], (B, S, E), dtype=jnp.float32)
        w_in = jax.random.uniform(ks[1], (3 * E, E), dtype=jnp.float32, minval=-scale, maxval=scale)
        b_in = jnp.zeros((3 * E,), dtype=jnp.float32)
        w_out = jax.random.uniform(ks[2], (E, E), dtype=jnp.float32, minval=-scale, maxval=scale)
        b_out = jnp.zeros((E,), dtype=jnp.float32)
        return {'x': x, 'w_in': w_in, 'b_in': b_in, 'w_out': w_out, 'b_out': b_out}
    _L1_attn_all = _L1_attn_setup()
    _L1_attn_in = {k: v for k, v in _L1_attn_all.items() if k in ('w_in', 'b_in', 'w_out', 'b_out')}
    del _L1_attn_all

    def _L1_xattn_setup():
        import jax, jax.numpy as jnp
        import numpy as np
        import math
        B, S, D, H = (4, 256, 128, 16)
        DK = D // H

        def _split_heads(x):
            b, s, _ = x.shape
            return x.reshape(b, s, H, DK).transpose(0, 2, 1, 3)
        key = jax.random.key(seed)
        ks = jax.random.split(key, 12)
        s = 1.0 / math.sqrt(D)
        inp = {'query': jax.random.normal(ks[0], (B, S, D), jnp.float32), 'key': jax.random.normal(ks[1], (B, S, D), jnp.float32), 'value': jax.random.normal(ks[2], (B, S, D), jnp.float32), 'mask': jnp.tril(jnp.ones((S, S), jnp.int32))[None, None, :, :], 'Wq': jax.random.normal(ks[3], (D, D), jnp.float32) * s, 'bq': jnp.zeros((D,), jnp.float32), 'Wk': jax.random.normal(ks[4], (D, D), jnp.float32) * s, 'bk': jnp.zeros((D,), jnp.float32), 'Wv': jax.random.normal(ks[5], (D, D), jnp.float32) * s, 'bv': jnp.zeros((D,), jnp.float32), 'Wo': jax.random.normal(ks[6], (D, D), jnp.float32) * s, 'bo': jnp.zeros((D,), jnp.float32)}
        return inp
    _L1_xattn_all = _L1_xattn_setup()
    _L1_xattn_in = {k: v for k, v in _L1_xattn_all.items() if k in ('Wq', 'bq', 'Wk', 'bk', 'Wv', 'bv', 'Wo', 'bo')}
    del _L1_xattn_all

    def _L1_ffn_setup():
        import jax, jax.numpy as jnp
        import numpy as np
        B, S, HID, DFF, E, K = (4, 256, 128, 512, 8, 256)
        key = jax.random.key(seed)
        ks = jax.random.split(key, 4)
        sc_h = 1.0 / np.sqrt(HID)
        sc_f = 1.0 / np.sqrt(DFF)
        return {'x': jax.random.normal(ks[0], (B, S, HID), jnp.float32), 'router_w': jax.random.normal(ks[1], (HID, E), jnp.float32) * sc_h, 'router_b': jnp.zeros((E,), jnp.float32), 'w1': jax.random.normal(ks[2], (E, HID, DFF), jnp.float32) * sc_h, 'b1': jnp.zeros((E, DFF), jnp.float32), 'w2': jax.random.normal(ks[3], (E, DFF, HID), jnp.float32) * sc_f, 'b2': jnp.zeros((E, HID), jnp.float32)}
    _L1_ffn_all = _L1_ffn_setup()
    _L1_ffn_in = {k: v for k, v in _L1_ffn_all.items() if k in ('router_w', 'router_b', 'w1', 'b1', 'w2', 'b2')}
    del _L1_ffn_all
    return {'x': x, 'ctx_1024': ctx_1024, 'mask_Bx1x1xS2_if1': mask_Bx1x1xS2_if1, 'mask_1x1xSxS2_ik0': mask_1x1xSxS2_ik0, 'L0_attn_Wq': _L0_attn_in['Wq'], 'L0_attn_Wk': _L0_attn_in['Wk'], 'L0_attn_Wv': _L0_attn_in['Wv'], 'L0_attn_Wo': _L0_attn_in['Wo'], 'L0_attn_bo': _L0_attn_in['bo'], 'L0_xattn_s_wq': _L0_xattn_in['s_wq'], 'L0_xattn_s_bq': _L0_xattn_in['s_bq'], 'L0_xattn_s_wk': _L0_xattn_in['s_wk'], 'L0_xattn_s_bk': _L0_xattn_in['s_bk'], 'L0_xattn_s_wv': _L0_xattn_in['s_wv'], 'L0_xattn_s_bv': _L0_xattn_in['s_bv'], 'L0_xattn_s_wo': _L0_xattn_in['s_wo'], 'L0_xattn_s_bo': _L0_xattn_in['s_bo'], 'L0_xattn_c_wq': _L0_xattn_in['c_wq'], 'L0_xattn_c_bq': _L0_xattn_in['c_bq'], 'L0_xattn_c_wk': _L0_xattn_in['c_wk'], 'L0_xattn_c_bk': _L0_xattn_in['c_bk'], 'L0_xattn_c_wv': _L0_xattn_in['c_wv'], 'L0_xattn_c_bv': _L0_xattn_in['c_bv'], 'L0_xattn_c_wo': _L0_xattn_in['c_wo'], 'L0_xattn_c_bo': _L0_xattn_in['c_bo'], 'L0_xattn_ff_w1': _L0_xattn_in['ff_w1'], 'L0_xattn_ff_b1': _L0_xattn_in['ff_b1'], 'L0_xattn_ff_w2': _L0_xattn_in['ff_w2'], 'L0_xattn_ff_b2': _L0_xattn_in['ff_b2'], 'L0_xattn_ln1_g': _L0_xattn_in['ln1_g'], 'L0_xattn_ln1_b': _L0_xattn_in['ln1_b'], 'L0_xattn_ln2_g': _L0_xattn_in['ln2_g'], 'L0_xattn_ln2_b': _L0_xattn_in['ln2_b'], 'L0_xattn_ln3_g': _L0_xattn_in['ln3_g'], 'L0_xattn_ln3_b': _L0_xattn_in['ln3_b'], 'L0_ffn_group_centroids': _L0_ffn_in['group_centroids'], 'L0_ffn_expert_centroids': _L0_ffn_in['expert_centroids'], 'L0_ffn_bias': _L0_ffn_in['bias'], 'L0_ffn_wg': _L0_ffn_in['wg'], 'L0_ffn_wu': _L0_ffn_in['wu'], 'L0_ffn_wd': _L0_ffn_in['wd'], 'L0_ffn_sg': _L0_ffn_in['sg'], 'L0_ffn_su': _L0_ffn_in['su'], 'L0_ffn_sd': _L0_ffn_in['sd'], 'L1_attn_w_in': _L1_attn_in['w_in'], 'L1_attn_b_in': _L1_attn_in['b_in'], 'L1_attn_w_out': _L1_attn_in['w_out'], 'L1_attn_b_out': _L1_attn_in['b_out'], 'L1_xattn_Wq': _L1_xattn_in['Wq'], 'L1_xattn_bq': _L1_xattn_in['bq'], 'L1_xattn_Wk': _L1_xattn_in['Wk'], 'L1_xattn_bk': _L1_xattn_in['bk'], 'L1_xattn_Wv': _L1_xattn_in['Wv'], 'L1_xattn_bv': _L1_xattn_in['bv'], 'L1_xattn_Wo': _L1_xattn_in['Wo'], 'L1_xattn_bo': _L1_xattn_in['bo'], 'L1_ffn_router_w': _L1_ffn_in['router_w'], 'L1_ffn_router_b': _L1_ffn_in['router_b'], 'L1_ffn_w1': _L1_ffn_in['w1'], 'L1_ffn_b1': _L1_ffn_in['b1'], 'L1_ffn_w2': _L1_ffn_in['w2'], 'L1_ffn_b2': _L1_ffn_in['b2']}

def reference(x, ctx_1024, mask_Bx1x1xS2_if1, mask_1x1xSxS2_ik0, L0_attn_Wq, L0_attn_Wk, L0_attn_Wv, L0_attn_Wo, L0_attn_bo, L0_xattn_s_wq, L0_xattn_s_bq, L0_xattn_s_wk, L0_xattn_s_bk, L0_xattn_s_wv, L0_xattn_s_bv, L0_xattn_s_wo, L0_xattn_s_bo, L0_xattn_c_wq, L0_xattn_c_bq, L0_xattn_c_wk, L0_xattn_c_bk, L0_xattn_c_wv, L0_xattn_c_bv, L0_xattn_c_wo, L0_xattn_c_bo, L0_xattn_ff_w1, L0_xattn_ff_b1, L0_xattn_ff_w2, L0_xattn_ff_b2, L0_xattn_ln1_g, L0_xattn_ln1_b, L0_xattn_ln2_g, L0_xattn_ln2_b, L0_xattn_ln3_g, L0_xattn_ln3_b, L0_ffn_group_centroids, L0_ffn_expert_centroids, L0_ffn_bias, L0_ffn_wg, L0_ffn_wu, L0_ffn_wd, L0_ffn_sg, L0_ffn_su, L0_ffn_sd, L1_attn_w_in, L1_attn_b_in, L1_attn_w_out, L1_attn_b_out, L1_xattn_Wq, L1_xattn_bq, L1_xattn_Wk, L1_xattn_bk, L1_xattn_Wv, L1_xattn_bv, L1_xattn_Wo, L1_xattn_bo, L1_ffn_router_w, L1_ffn_router_b, L1_ffn_w1, L1_ffn_b1, L1_ffn_w2, L1_ffn_b2):
    import jax
    import jax.numpy as jnp

    def _L0_attn_ref(x, Wq, Wk, Wv, Wo, bo):
        import jax, jax.numpy as jnp
        import numpy as np
        NUM_HEADS = 16
        b, s, d = x.shape
        h = NUM_HEADS
        hd = d // h
        q = (x @ Wq).reshape(b, s, h, hd).transpose(0, 2, 1, 3)
        k = (x @ Wk).reshape(b, s, h, hd).transpose(0, 2, 1, 3)
        v = (x @ Wv).reshape(b, s, h, hd).transpose(0, 2, 1, 3)
        scores = jnp.einsum('bhqd,bhkd->bhqk', q, k)
        causal = jnp.arange(s)[:, None] >= jnp.arange(s)[None, :]
        scores = jnp.where(causal[None, None], scores, -jnp.inf)
        attn = jax.nn.softmax(scores / np.sqrt(hd), axis=-1)
        ctx = jnp.einsum('bhqk,bhkd->bhqd', attn, v)
        ctx = ctx.transpose(0, 2, 1, 3).reshape(b, s, d)
        return ctx @ Wo + bo

    def _L0_xattn_ref(x, encoder_output, src_mask, tgt_mask, s_wq, s_bq, s_wk, s_bk, s_wv, s_bv, s_wo, s_bo, c_wq, c_bq, c_wk, c_bk, c_wv, c_bv, c_wo, c_bo, ff_w1, ff_b1, ff_w2, ff_b2, ln1_g, ln1_b, ln2_g, ln2_b, ln3_g, ln3_b):
        import jax, jax.numpy as jnp
        import numpy as np
        import math
        D, NH, DFF = (128, 16, 512)
        B, S = (2, 256)
        EPS = 1e-05

        def _mha(q_in, k_in, v_in, wq, bq, wk, bk, wv, bv, wo, bo, mask):
            Bq, Sq, Dm = q_in.shape
            Sk = k_in.shape[1]
            dh = Dm // NH
            q = (q_in @ wq + bq).reshape(Bq, Sq, NH, dh).transpose(0, 2, 1, 3)
            k = (k_in @ wk + bk).reshape(Bq, Sk, NH, dh).transpose(0, 2, 1, 3)
            v = (v_in @ wv + bv).reshape(Bq, Sk, NH, dh).transpose(0, 2, 1, 3)
            scores = jnp.einsum('bhqd,bhkd->bhqk', q, k) / math.sqrt(dh)
            scores = jnp.where(mask == 0, jnp.float32(-1000000000.0), scores)
            w = jax.nn.softmax(scores, axis=-1)
            out = jnp.einsum('bhqk,bhkd->bhqd', w, v)
            out = out.transpose(0, 2, 1, 3).reshape(Bq, Sq, Dm)
            return out @ wo + bo

        def _ln(x, g, b):
            mu = jnp.mean(x, axis=-1, keepdims=True)
            var = jnp.var(x, axis=-1, keepdims=True)
            return (x - mu) * jax.lax.rsqrt(var + EPS) * g + b
        a = _mha(x, x, x, s_wq, s_bq, s_wk, s_bk, s_wv, s_bv, s_wo, s_bo, tgt_mask)
        x = _ln(x + a, ln1_g, ln1_b)
        a = _mha(x, encoder_output, encoder_output, c_wq, c_bq, c_wk, c_bk, c_wv, c_bv, c_wo, c_bo, src_mask)
        x = _ln(x + a, ln2_g, ln2_b)
        f = jax.nn.relu(x @ ff_w1 + ff_b1) @ ff_w2 + ff_b2
        return _ln(x + f, ln3_g, ln3_b)

    def _L0_ffn_ref(x, group_centroids, expert_centroids, bias, wg, wu, wd, sg, su, sd):
        import jax, jax.numpy as jnp
        import numpy as np
        B, S, D = (2, 256, 128)
        E, G, K = (32, 8, 4)
        H, SH = (256, 256)
        CAP_FACTOR = 1.25

        def _l2norm(v):
            n = jnp.linalg.norm(v, axis=-1, keepdims=True)
            return v / jnp.maximum(n, 1e-12)
        b, s, d = x.shape
        xf = x.reshape(-1, d)
        N = xf.shape[0]
        shared = jax.nn.silu(xf @ sg) * (xf @ su) @ sd
        xn = _l2norm(xf)
        group_scores = xn @ _l2norm(group_centroids).T
        n_top_groups = max(1, G // 2)
        _, top_group_idx = jax.lax.top_k(group_scores, n_top_groups)
        expert_scores = xn @ _l2norm(expert_centroids).T + bias
        expert_to_group = jnp.arange(E) // (E // G)
        sel = jnp.zeros((N, G), xf.dtype).at[jnp.arange(N)[:, None], top_group_idx].set(1.0)
        group_mask = sel[:, expert_to_group]
        masked = expert_scores * group_mask + (1.0 - group_mask) * -1000000000.0
        top_scores, top_idx = jax.lax.top_k(masked, K)
        gates = jax.nn.softmax(top_scores, axis=-1)
        capacity = max(1, int(N / E * K * CAP_FACTOR))
        flat_e = top_idx.reshape(-1)
        flat_g = gates.reshape(-1)
        tok = jnp.repeat(jnp.arange(N), K)
        onehot = jax.nn.one_hot(flat_e, E, dtype=jnp.int32)
        pos = jnp.cumsum(onehot, axis=0)[jnp.arange(N * K), flat_e] - 1
        keep = pos < capacity
        e_s = jnp.where(keep, flat_e, E)
        p_s = jnp.where(keep, pos, 0)
        buf = jnp.zeros((E + 1, capacity, d), xf.dtype).at[e_s, p_s].set(xf[tok])[:E]
        h = jax.nn.silu(jnp.einsum('ecd,edh->ech', buf, wg)) * jnp.einsum('ecd,edh->ech', buf, wu)
        out_e = jnp.einsum('ech,ehd->ecd', h, wd)
        gathered = out_e[flat_e, jnp.minimum(pos, capacity - 1)]
        contrib = gathered * (flat_g * keep.astype(xf.dtype))[:, None]
        routed = jnp.zeros_like(xf).at[tok].add(contrib)
        return (shared + routed).reshape(b, s, d)

    def _L1_attn_ref(x, w_in, b_in, w_out, b_out):
        import jax, jax.numpy as jnp
        import numpy as np
        B, S, E, H, W = (4, 256, 128, 16, 128)
        HD = E // H
        b, s, e = x.shape
        qkv = x @ w_in.T + b_in
        q, k, v = jnp.split(qkv, 3, axis=-1)
        q = q.reshape(b, s, H, HD).transpose(0, 2, 1, 3)
        k = k.reshape(b, s, H, HD).transpose(0, 2, 1, 3)
        v = v.reshape(b, s, H, HD).transpose(0, 2, 1, 3)
        scores = jnp.einsum('bhqd,bhkd->bhqk', q, k) / jnp.sqrt(jnp.asarray(HD, x.dtype))
        i = jnp.arange(s)[:, None]
        j = jnp.arange(s)[None, :]
        allowed = (j <= i) & (j >= i - W)
        scores = jnp.where(allowed[None, None], scores, jnp.asarray(-1000000000.0, x.dtype))
        attn = jax.nn.softmax(scores, axis=-1)
        out = jnp.einsum('bhqk,bhkd->bhqd', attn, v)
        out = out.transpose(0, 2, 1, 3).reshape(b, s, e)
        return out @ w_out.T + b_out

    def _L1_xattn_ref(query, key, value, mask, Wq, bq, Wk, bk, Wv, bv, Wo, bo):
        import jax, jax.numpy as jnp
        import numpy as np
        import math
        B, S, D, H = (4, 256, 128, 16)
        DK = D // H

        def _split_heads(x):
            b, s, _ = x.shape
            return x.reshape(b, s, H, DK).transpose(0, 2, 1, 3)
        q = _split_heads(query @ Wq.T + bq)
        k = _split_heads(key @ Wk.T + bk)
        v = _split_heads(value @ Wv.T + bv)
        scores = jnp.einsum('bhqd,bhkd->bhqk', q, k) / math.sqrt(DK)
        scores = jnp.where(mask == 0, jnp.float32(-1000000000.0), scores)
        probs = jax.nn.softmax(scores, axis=-1)
        x = jnp.einsum('bhqk,bhkd->bhqd', probs, v)
        x = x.transpose(0, 2, 1, 3).reshape(query.shape[0], query.shape[1], D)
        return x @ Wo.T + bo

    def _L1_ffn_ref(x, router_w, router_b, w1, b1, w2, b2):
        import jax, jax.numpy as jnp
        import numpy as np
        B, S, HID, DFF, E, K = (4, 256, 128, 512, 8, 256)
        b, s, h = x.shape
        xf = x.reshape(-1, h)
        logits = xf @ router_w + router_b
        scores = jax.nn.softmax(logits, axis=-1)
        G, idx = jax.lax.top_k(scores.T, K)
        toks = xf[idx]
        h1 = jax.nn.relu(jnp.einsum('ekh,ehf->ekf', toks, w1) + b1[:, None, :])
        eo = jnp.einsum('ekf,efh->ekh', h1, w2) + b2[:, None, :]
        contrib = (eo * G[..., None]).reshape(-1, h)
        y = jnp.zeros_like(xf).at[idx.reshape(-1)].add(contrib)
        return y.reshape(b, s, h)
    x = _layernorm(x + _L0_attn_ref(x, L0_attn_Wq, L0_attn_Wk, L0_attn_Wv, L0_attn_Wo, L0_attn_bo), axis=-1)
    x = _layernorm(x + _L0_xattn_ref(x, ctx_1024, mask_Bx1x1xS2_if1, mask_1x1xSxS2_ik0, L0_xattn_s_wq, L0_xattn_s_bq, L0_xattn_s_wk, L0_xattn_s_bk, L0_xattn_s_wv, L0_xattn_s_bv, L0_xattn_s_wo, L0_xattn_s_bo, L0_xattn_c_wq, L0_xattn_c_bq, L0_xattn_c_wk, L0_xattn_c_bk, L0_xattn_c_wv, L0_xattn_c_bv, L0_xattn_c_wo, L0_xattn_c_bo, L0_xattn_ff_w1, L0_xattn_ff_b1, L0_xattn_ff_w2, L0_xattn_ff_b2, L0_xattn_ln1_g, L0_xattn_ln1_b, L0_xattn_ln2_g, L0_xattn_ln2_b, L0_xattn_ln3_g, L0_xattn_ln3_b), axis=-1)
    x = _layernorm(x + _L0_ffn_ref(x, L0_ffn_group_centroids, L0_ffn_expert_centroids, L0_ffn_bias, L0_ffn_wg, L0_ffn_wu, L0_ffn_wd, L0_ffn_sg, L0_ffn_su, L0_ffn_sd), axis=-1)
    x = _layernorm(x + _L1_attn_ref(x, L1_attn_w_in, L1_attn_b_in, L1_attn_w_out, L1_attn_b_out), axis=-1)
    x = _layernorm(x + _L1_xattn_ref(x, ctx_1024, ctx_1024, mask_1x1xSxS2_ik0, L1_xattn_Wq, L1_xattn_bq, L1_xattn_Wk, L1_xattn_bk, L1_xattn_Wv, L1_xattn_bv, L1_xattn_Wo, L1_xattn_bo), axis=-1)
    x = _layernorm(x + _L1_ffn_ref(x, L1_ffn_router_w, L1_ffn_router_b, L1_ffn_w1, L1_ffn_b1, L1_ffn_w2, L1_ffn_b2), axis=-1)
    return x

_drawn_inputs = setup_inputs


def setup_inputs(seed=0):
    import zlib

    import numpy as np

    out = dict(_drawn_inputs(seed))
    spreads = {'L0_attn_bo': (0.0, 0.1),
     'L0_xattn_s_bq': (0.0, 0.1),
     'L0_xattn_s_bk': (0.0, 0.8),
     'L0_xattn_s_bv': (0.0, 0.1),
     'L0_xattn_s_bo': (0.0, 0.1),
     'L0_xattn_c_bq': (0.0, 0.1),
     'L0_xattn_c_bk': (0.0, 0.8),
     'L0_xattn_c_bv': (0.0, 0.1),
     'L0_xattn_c_bo': (0.0, 0.1),
     'L0_xattn_ff_b1': (0.0, 0.1),
     'L0_xattn_ff_b2': (0.0, 0.1),
     'L0_xattn_ln1_g': (1.0, 0.2),
     'L0_xattn_ln1_b': (0.0, 0.1),
     'L0_xattn_ln2_g': (1.0, 0.2),
     'L0_xattn_ln2_b': (0.0, 0.1),
     'L0_xattn_ln3_g': (1.0, 0.2),
     'L0_xattn_ln3_b': (0.0, 0.1),
     'L0_ffn_bias': (0.0, 0.1),
     'L1_attn_b_in': (0.0, 0.1),
     'L1_attn_b_out': (0.0, 0.1),
     'L1_xattn_bq': (0.0, 0.1),
     'L1_xattn_bk': (0.0, 0.8),
     'L1_xattn_bv': (0.0, 0.1),
     'L1_xattn_bo': (0.0, 0.1),
     'L1_ffn_router_b': (0.0, 0.1),
     'L1_ffn_b1': (0.0, 0.269),
     'L1_ffn_b2': (0.0, 0.1)}
    factors = {}
    for name, (base, spread) in spreads.items():
        noise = np.random.default_rng([zlib.crc32(name.encode()), seed]).standard_normal(out[name].shape)
        drawn = base * np.exp(spread * noise) if base else spread * noise
        out[name] = jnp.asarray(drawn.astype(out[name].dtype))
    for name, factor in factors.items():
        out[name] = (out[name] * factor).astype(out[name].dtype)
    return out
```

```python
from contextlib import ExitStack

import concourse.bass as bass
from concourse import mybir

ALU = mybir.AluOpType
ACT = mybir.ActivationFunctionType
AX = mybir.AxisListType.X
F32 = mybir.dt.float32
BF16 = mybir.dt.bfloat16
I32 = mybir.dt.int32
U32 = mybir.dt.uint32

P = 128
B, S, D = 4, 256, 128
NT = B * S // P
NH, DH = 16, 8
QB = S // P
SCALE = float(DH) ** -0.5
EPS = 1e-5
MASKED = -(2.0 ** 60)
DFF = 512
NF = DFF // P

PAIRS = [(0, 0), (0, 1), (0, 2), (1, 0), (1, 1), (2, 0)]
QRUNS = [(0, 3, 0), (3, 2, 1), (5, 1, 2)]
MASK_ROW = DH * len(PAIRS)
KEY_ROWS = 66
MAX_ROW = KEY_ROWS
ALL_ROWS = MAX_ROW + 3

NLAYER = 5
NSTEP = NLAYER * B
CAUSAL, GIVEN, KEYS, WINDOW = range(4)
KIND = [CAUSAL, GIVEN, KEYS, WINDOW, GIVEN]
CROSS = [False, False, True, False, True]
SEGMENTS = [(0, 3 * B), (3 * B, NSTEP)]
AFFINE = {1: 0, 2: 1}

E0, G0, K0, H0 = 32, 8, 4, 256
CAP = max(1, int(B * S / E0 * K0 * 1.25))
SLOTS = E0 * CAP
ST = SLOTS // P
HC = CAP // 2
BITS = 30
FAR = 1.0e6
GRP = 2
NGRP = E0 // GRP
WRING = 3
E1, K1 = 8, 256


def build(nc: bass.Bass, a, out, last_stage=9):
    ctx = ExitStack()
    with ctx:
        def sb(name, shape, dt=F32):
            return ctx.enter_context(nc.sbuf_tensor(name, shape, dt))

        def pb(name, shape, dt=F32):
            return ctx.enter_context(nc.psum_tensor(name, shape, dt))

        def sem(name):
            return ctx.enter_context(nc.semaphore(name))

        def dram(name, shape, dt=F32):
            return nc.dram_tensor(name, shape, dt, kind="Internal").ap()

        q_parts_dram = dram("q_parts_dram", (2, 3, P, S), BF16)
        k_parts_dram = dram("k_parts_dram", (2, 3, P, S), BF16)
        key_mask_dram = dram("key_mask_dram", (B + 1, S), BF16)
        slot_x_dram = dram("slot_x_dram", (SLOTS, D))
        slot_y_dram = dram("slot_y_dram", (SLOTS, D))

        X = sb("X", [P, NT, D])
        XI = sb("XI", [P, NT, D])
        ctx_rows = sb("ctx_rows", [P, NT, D])
        ctxT = sb("ctxT", [P, B, S])
        xT = sb("xT", [P, 2, S])
        ident = sb("ident", [P, P])
        ident_b = sb("ident_b", [P, P], BF16)
        tri = sb("tri", [P, 2, P], BF16)
        given = sb("given", [P, QB, S], BF16)
        givenT = sb("givenT", [P, QB, S], BF16)
        given_i = sb("given_i", [P, QB, S], I32)
        keys_i = sb("keys_i", [B, S], I32)
        keys_row = sb("keys_row", [B + 1, S], BF16)
        neg_half = sb("neg_half", [P, NT])
        Wq = sb("Wq", [P, NLAYER, D])
        Wk = sb("Wk", [P, NLAYER, D])
        Wv = sb("Wv", [P, NLAYER, D])
        Wo = sb("Wo", [P, NLAYER, D])
        w_rows = sb("w_rows", [P, 8, D])
        bqk = sb("bqk", [P, NLAYER, 2])
        bvo = sb("bvo", [P, NLAYER, 2, D])
        ln_gb = sb("ln_gb", [P, 3, 2, D])
        stackQ = sb("stackQ", [ALL_ROWS, 3, NH, S], BF16)
        stackK = sb("stackK", [ALL_ROWS, 3, NH, S], BF16)
        q_parts = sb("q_parts", [P, 2, 3, S], BF16)
        k_parts = sb("k_parts", [P, 2, 3, S], BF16)
        q_rest = sb("q_rest", [P, 2, S])
        k_rest = sb("k_rest", [P, 2, S])
        v_aug = sb("v_aug", [P, 3, QB, NH, 32])
        mx = sb("mx", [P, QB, NH])
        m_rest = sb("m_rest", [P, 2, QB, NH])
        m_parts = sb("m_parts", [P, 2, QB, 3, NH], BF16)
        mT = sb("mT", [3 * NH, 2, S], BF16)
        arena = sb("arena", [P, 6 * 4 * S])
        probsT = arena[:, 0:3 * 4 * S].rearrange("p (n j q) -> p n j q", n=3, j=4)
        oT = arena[:, 3 * 4 * S:4 * 4 * S].rearrange("p (n g q) -> p n g q", n=2, g=2)
        inv_den = sb("inv_den", [P, 2, QB, 8])
        o_rows = sb("o_rows", [P, 2, QB, D])
        nT = sb("nT", [P, 2, S])
        res = sb("res", [P, 2, QB, D])
        stats = sb("stats", [P, 2, QB, 6])
        mv = sb("mv", [P, 2, QB, 2])
        var_eps = sb("var_eps", [P, 2, QB])
        rstd = sb("rstd", [P, 2, QB])

        ff_w1 = sb("ff_w1", [P, DFF])
        ff_w2 = sb("ff_w2", [P, NF, D])
        ff_b1 = sb("ff_b1", [P, NF])
        ff_b2 = sb("ff_b2", [P, D])
        ff_h = arena[:, 4 * 4 * S:6 * 4 * S].rearrange("p (n f q) -> p n f q", n=2, f=NF)
        xT_all = sb("xT_all", [P, B * S])
        cent = sb("cent", [G0 + E0, D])
        cent_sq = sb("cent_sq", [G0 + E0, D])
        cent_n = sb("cent_n", [G0 + E0, 2])
        centT = sb("centT", [P, G0 + E0])
        bias0 = sb("bias0", [P, E0])
        sq = w_rows[:, :, :]
        norm_x = sb("norm_x", [P, 2, NT])
        scs = sb("scs", [P, NT, G0 + E0])
        g_gt = sb("g_gt", [P, NT, G0, G0])
        g_eq = sb("g_eq", [P, NT, G0, G0])
        lower = sb("lower", [P, G0, G0])
        g_rank = sb("g_rank", [P, NT, G0])
        g_in = sb("g_in", [P, NT, G0])
        g_pen = sb("g_pen", [P, NT, G0])
        top_v = sb("top_v", [P, NT, 8])
        top_i = sb("top_i", [P, NT, 8], U32)
        top_f = sb("top_f", [P, NT, K0])
        gate = sb("gate", [P, NT, K0])
        gate_sum = sb("gate_sum", [P, 2, NT])
        iota_e = sb("iota_e", [P, E0])
        hot = sb("hot", [P, NT * K0, E0])
        hot_pos = w_rows[:, :, :].rearrange("p a (b e) -> p (a b) e", e=E0)
        chosen = sb("chosen", [P, NT, E0], BF16)
        before_b = sb("before_b", [P, P], BF16)
        ones_b = sb("ones_b", [P, P], BF16)
        pos = sb("pos", [P, NT * K0])
        over = sb("over", [P, NT * K0])
        slot = sb("slot", [P, 3, NT * K0])
        slot_to = sb("slot_to", [P, NT * K0], U32)
        slot_from = sb("slot_from", [P, NT * K0], U32)
        sh_g = sb("sh_g", [P, H0])
        sh_u = sb("sh_u", [P, H0])
        sh_d = sb("sh_d", [P, 2, D])
        slot_rows = sb("slot_rows", [P, 2, 8, D])
        slotT = arena[:, 0:SLOTS]
        y_chosen = arena[:, 0:NT * K0 * D].rearrange("p (j d) -> p j d", d=D)
        silu_e = arena[:, SLOTS:SLOTS + 4 * CAP].rearrange("p (n c) -> p n c", n=2)
        silu_sh = arena[:, 2 * B * S:4 * B * S].rearrange("p (c h n) -> p c h n", c=2, h=2)
        wg_b = sb("wg_b", [P, WRING, GRP, H0])
        wu_b = sb("wu_b", [P, WRING, GRP, H0])
        wd_b = sb("wd_b", [P, WRING, GRP, 2, D])
        hT = sb("hT", [P, 2, 2, CAP])
        y_rows = sb("y_rows", [HC, 2, 2, D])
        Y = ctx_rows
        w1_b = wg_b[:, :, :, :].rearrange("p r e n -> p r (e n)")
        w2_b = wd_b[:, :, :, :, :].rearrange("p r e h d -> p r (e h) d")
        h1 = arena[:, 0:8 * 512].rearrange("p (n f t) -> p n f t", n=2, f=NF)
        router = sb("router", [P, E1])
        router_bias = sb("router_bias", [P, E1])
        b1_rows = sb("b1_rows", [E1 * NF, P])
        b1_cols = sb("b1_cols", [P, E1 * NF])
        b2_rows = sb("b2_rows", [E1, D])
        G = sb("G", [P, NT, E1])
        g_top = sb("g_top", [P, NT])
        flag = sb("flag", [P, 2, NT, E1])
        flag_sum = sb("flag_sum", [P, E1], BF16)
        equal = sb("equal", [P, NT, E1], BF16)
        low_cut = sb("low_cut", [P, E1])
        try_cut = sb("try_cut", [P, E1])
        try_ok = sb("try_ok", [P, E1])
        wT = slot_rows[0:E1, 0, :, :].rearrange("p t d -> p (t d)")
        psM = pb("psM", [P, 2, 512])
        psE = pb("psE", [P, 2, 1024])
        psO = pb("psO", [P, 2, S])
        psX = pb("psX", [P, 2, S])
        psA, psB = psX[:, 0, :], psX[:, 1, :]

        pos_ps = psX[:, :, :].rearrange("p a n -> p (a n)")[:, 0:NT * E0].rearrange("p (t e) -> p t e", t=NT)
        rs_ps = psX[:, :, :].rearrange("p a n -> p (a n)")[:, 0:NT * (G0 + E0)].rearrange("p (t e) -> p t e", t=NT)
        psE4 = psE[:, :, :].rearrange("p a n -> p (a n)").rearrange("p (f n) -> p f n", f=4)
        sh_hT = slotT[:, 0:2 * B * S].rearrange("p (h t) -> p h t", h=2)

        names = {}

        def s_(name):
            if name not in names:
                names[name] = sem(name)
            return names[name]

        const_ready = s_("const_ready")
        x_loaded, ctx_loaded, w_loaded, wr_loaded, mask_loaded = map(s_, (
            "x_loaded", "ctx_loaded", "w_loaded", "wr_loaded", "mask_loaded"))
        keys_made, keys_stored, given_made, setup_pe, setup_act = map(s_, (
            "keys_made", "keys_stored", "given_made", "setup_pe", "setup_act"))
        x_ready = s_("x_ready")
        t_done, xT_ready, q_done, k_done, v_done, q_hi, k_hi = map(s_, (
            "t_done", "xT_ready", "q_done", "k_done", "v_done", "q_hi", "k_hi"))
        q_resid, k_resid, v_ready, q_split, k_split = map(s_, (
            "q_resid", "k_resid", "v_ready", "q_split", "k_split"))
        q_stored, k_stored = map(s_, ("q_stored", "k_stored"))
        stack_loaded = [s_(f"stack_loaded{j}") for j in range(3)]
        m_loaded = [s_(f"m_loaded{j}") for j in range(2)]
        m_full, m_used, mx_done, m_split, mt_done, mT_ready = map(s_, (
            "m_full", "m_used", "mx_done", "m_split", "mt_done", "mT_ready"))
        e_full, exp_done, pv_done, oT_ready = map(s_, ("e_full", "exp_done", "pv_done", "oT_ready"))
        nt_done, nT_ready, wo_done, wo_read = map(s_, (
            "nt_done", "nT_ready", "wo_done", "wo_read"))
        pool_chain, dve_chain, rstd_ready, var_ready = map(s_, ("pool_chain", "dve_chain", "rstd_ready", "var_ready"))
        out_stored = s_("out_stored")

        f_xT, f_turned, f_up, f_h, f_down, f_read, ff_loaded = map(s_, (
            "f_xT", "f_turned", "f_up", "f_h", "f_down", "f_read", "ff_loaded"))
        x3_ready, moe0_ready, r_loaded, zero_ready, zero_stored = map(s_, (
            "x3_ready", "moe0_ready", "r_loaded", "zero_ready", "zero_stored"))
        xa_turned, xa_ready, cent_turned, centT_ready, cent_ready, rscore_done, rscore_read = map(s_, (
            "xa_turned", "xa_ready", "cent_turned", "centT_ready", "cent_ready", "rscore_done", "rscore_read"))
        pow_in, pow_out, gate_in, gate_exp, chosen_ready, pos_done, slots_ready, scattered = map(s_, (
            "pow_in", "pow_out", "gate_in", "gate_exp", "chosen_ready", "pos_done", "slots_ready", "scattered"))
        sh_up, sh_silu, sh_h, sh_down, sh_read = map(s_, ("sh_up", "sh_silu", "sh_h", "sh_down", "sh_read"))
        slots_loaded = [s_(f"slots_loaded{j}") for j in range(ST // 8)]
        slots_turned, slotT_ready = s_("slots_turned"), s_("slotT_ready")
        we_loaded = [s_(f"we_loaded{j}") for j in range(WRING)]
        e_up, e_silu, e_h, e_down, e_rows = map(s_, ("e_up", "e_silu", "e_h", "e_down", "e_rows"))
        y_stored = [s_(f"y_stored{j}") for j in range(2)]
        gathered = [s_(f"gathered{j}") for j in range(NT)]

        m1_loaded, l_done, l_exp_in, l_exp, b1_turned, b1_ready, try_ready, try_counted = map(s_, (
            "m1_loaded", "l_done", "l_exp_in", "l_exp", "b1_turned", "b1_ready", "try_ready", "try_counted"))
        eq_ready, eq_ranked, w_ready, w_turned, wT_ready, b2_done, b2_read = map(s_, (
            "eq_ready", "eq_ranked", "w_ready", "w_turned", "wT_ready", "b2_done", "b2_read"))
        w1_loaded = [s_(f"w1_loaded{j}") for j in range(WRING)]
        d_up, d_relu, d_down, d_read, final_ready = map(s_, ("d_up", "d_relu", "d_down", "d_read", "final_ready"))
        def x_in(layer):
            return XI if layer == 2 else X

        def x_out(layer):
            return XI if layer in (1, 2) else X

        def qlen(layer, kb):
            return kb if KIND[layer] in (CAUSAL, WINDOW) else 0

        def klen(layer, qb):
            return (qb + 1) * P if KIND[layer] in (CAUSAL, WINDOW) else S

        def m_order(lo, hi):
            for i in range(lo - 2, hi + 1):
                if lo <= i - 1 < hi:
                    yield ("o", i - 1, 1)
                if lo <= i + 1 < hi:
                    for c in range(16):
                        yield ("s", i + 1, c)
                if lo <= i < hi:
                    yield ("o", i, 0)

        m_at = {key: n for n, key in enumerate(k for lo, hi in SEGMENTS for k in m_order(lo, hi))}
        SCORES_PER_SLOT = [3, 3, 3, 3, 3, 1, 0, 0]

        chain_counts = {"dve": 0, "pool": 0}

        block = ctx.enter_context(nc.Block())

        W_NAMES = [("L0_attn_Wq", "L0_attn_Wk", "L0_attn_Wv", "L0_attn_Wo"),
                   ("L0_xattn_s_wq", "L0_xattn_s_wk", "L0_xattn_s_wv", "L0_xattn_s_wo"),
                   ("L0_xattn_c_wq", "L0_xattn_c_wk", "L0_xattn_c_wv", "L0_xattn_c_wo")]
        BIAS = {(1, 0): "L0_xattn_s_bq", (1, 1): "L0_xattn_s_bk", (1, 2): "L0_xattn_s_bv", (1, 3): "L0_xattn_s_bo",
                (2, 0): "L0_xattn_c_bq", (2, 1): "L0_xattn_c_bk", (2, 2): "L0_xattn_c_bv", (2, 3): "L0_xattn_c_bo",
                (0, 3): "L0_attn_bo", (3, 3): "L1_attn_b_out",
                (4, 0): "L1_xattn_bq", (4, 1): "L1_xattn_bk", (4, 2): "L1_xattn_bv", (4, 3): "L1_xattn_bo"}
        N_W = 12 + len(BIAS) + 3 + 6
        row = lambda v: v.rearrange("(a n) -> a n", a=1)
        col = lambda v: v.rearrange("(n a) -> n a", a=1)

        @block.sync
        def _(sp):
            xv = a["x"].rearrange("b (t p) d -> p (b t) d", p=P)
            sp.dma_start(X[:, :, :], xv).then_inc(x_loaded, 16)
            for w, name in zip((Wq, Wk, Wv, Wo), W_NAMES[0]):
                sp.dma_start(w[:, 0, :], a[name]).then_inc(w_loaded, 16)
            sp.dma_start(ctx_rows[:, :, :], a["ctx_1024"].rearrange("b (t p) d -> p (b t) d", p=P))\
                .then_inc(ctx_loaded, 16)
            for layer in (1, 2):
                for w, name in zip((Wq, Wk, Wv, Wo), W_NAMES[layer]):
                    sp.dma_start(w[:, layer, :], a[name]).then_inc(w_loaded, 16)
            for c in range(3):
                sp.dma_start(w_rows[:, c, :], a["L1_attn_w_in"][c * P:(c + 1) * P, :]).then_inc(wr_loaded, 16)
            sp.dma_start(w_rows[:, 3, :], a["L1_attn_w_out"]).then_inc(wr_loaded, 16)
            for c, name in enumerate(("L1_xattn_Wq", "L1_xattn_Wk", "L1_xattn_Wv", "L1_xattn_Wo")):
                sp.dma_start(w_rows[:, 4 + c, :], a[name]).then_inc(wr_loaded, 16)
            for (layer, c), name in BIAS.items():
                dst = bqk[:, layer, c:c + 1] if c < 2 else bvo[:, layer, c - 2, :]
                src = col(a[name]) if c < 2 else row(a[name]).broadcast_to([P, D])
                sp.dma_start(dst, src).then_inc(w_loaded, 16)
            b_in = a["L1_attn_b_in"]
            for c in range(2):
                sp.dma_start(bqk[:, 3, c:c + 1], col(b_in[c * P:(c + 1) * P])).then_inc(w_loaded, 16)
            sp.dma_start(bvo[:, 3, 0, :], row(b_in[2 * P:3 * P]).broadcast_to([P, D])).then_inc(w_loaded, 16)
            for n in range(3):
                for c, g in enumerate("gb"):
                    sp.dma_start(ln_gb[:, n, c, :], row(a[f"L0_xattn_ln{n + 1}_{g}"]).broadcast_to([P, D]))\
                        .then_inc(w_loaded, 16)
            sp.dma_start(ff_w1[:, :], a["L0_xattn_ff_w1"]).then_inc(ff_loaded, 16)
            sp.dma_start(ff_w2[:, :, :], a["L0_xattn_ff_w2"].rearrange("(f p) d -> p f d", p=P)).then_inc(ff_loaded, 16)
            for f in range(NF):
                sp.dma_start(ff_b1[:, f:f + 1], col(a["L0_xattn_ff_b1"][f * P:(f + 1) * P])).then_inc(ff_loaded, 16)
            sp.dma_start(ff_b2[:, :], row(a["L0_xattn_ff_b2"]).broadcast_to([P, D])).then_inc(ff_loaded, 16)
            sp.dma_start(router[:, :], a["L1_ffn_router_w"]).then_inc(m1_loaded, 16)
            sp.dma_start(router_bias[:, :], row(a["L1_ffn_router_b"]).broadcast_to([P, E1])).then_inc(m1_loaded, 16)
            sp.dma_start(b1_rows[:, :], a["L1_ffn_b1"].rearrange("e (f p) -> (e f) p", p=P)).then_inc(m1_loaded, 16)
            sp.dma_start(b2_rows[:, :], a["L1_ffn_b2"]).then_inc(m1_loaded, 16)
            sp.dma_start(cent[0:G0, :], a["L0_ffn_group_centroids"]).then_inc(r_loaded, 16)
            sp.dma_start(cent[G0:G0 + E0, :], a["L0_ffn_expert_centroids"]).then_inc(r_loaded, 16)
            sp.dma_start(bias0[:, :], row(a["L0_ffn_bias"]).broadcast_to([P, E0])).then_inc(r_loaded, 16)
            sp.dma_start(sh_g[:, :], a["L0_ffn_sg"]).then_inc(r_loaded, 16)
            sp.dma_start(sh_u[:, :], a["L0_ffn_su"]).then_inc(r_loaded, 16)
            sp.dma_start(sh_d[:, :, :], a["L0_ffn_sd"].rearrange("(h p) d -> p h d", p=P)).then_inc(r_loaded, 16)
            sp.wait_ge(keys_made, 1)
            sp.dma_start(key_mask_dram, keys_row[:, :]).then_inc(keys_stored, 16)
            sp.wait_ge(keys_stored, 16)

            sp.wait_ge(zero_ready, 1)
            for j in range(ST // 8):
                sp.dma_start(slot_x_dram[8 * j * P:8 * (j + 1) * P, :].rearrange("(p t) d -> p t d", p=P),
                             slot_rows[:, 0, :, :]).then_inc(zero_stored, 16)

            def load_experts(g):
                if g >= WRING:
                    sp.wait_ge(e_down, GRP * (g - WRING + 1))
                r, e = g % WRING, slice(GRP * g, GRP * (g + 1))
                sp.dma_start(wg_b[:, r, :, :], a["L0_ffn_wg"][e].rearrange("e d h -> d e h")).then_inc(we_loaded[r], 16)
                sp.dma_start(wu_b[:, r, :, :], a["L0_ffn_wu"][e].rearrange("e d h -> d e h")).then_inc(we_loaded[r], 16)
                sp.dma_start(wd_b[:, r, :, :, :], a["L0_ffn_wd"][e].rearrange("e (h p) d -> p e h d", p=P))\
                    .then_inc(we_loaded[r], 16)

            def first_mixture():
                for g in range(WRING):
                    load_experts(g)
                sp.wait_ge(scattered, 16 * NT * K0)
                for j in range(ST // 8):
                    if j >= 2:
                        sp.wait_ge(slots_turned, j - 1)
                    sp.dma_start(slot_rows[:, j % 2, :, :],
                                 slot_x_dram[8 * j * P:8 * (j + 1) * P, :].rearrange("(t p) d -> p t d", p=P))\
                        .then_inc(slots_loaded[j], 16)
                for e in range(E0):
                    sp.wait_ge(e_rows, e + 1)
                    sp.dma_start(slot_y_dram[e * CAP:(e + 1) * CAP, :].rearrange("(c p) d -> p c d", p=HC),
                                 y_rows[:, e % 2, :, :]).then_inc(y_stored[e % 2], 16)
                    if e % GRP == GRP - 1 and e // GRP + WRING < NGRP:
                        load_experts(e // GRP + WRING)

            def send_parts(n):
                buf, par, r = n % 3, n % 2, n % B if KIND[n // B] == KEYS else B
                sp.wait_ge(q_split, n + 1)
                sp.dma_start(q_parts_dram[par].rearrange("s p t -> p s t"), q_parts[:, par, :, :]).then_inc(q_stored, 16)
                sp.wait_ge(k_split, n + 1)
                sp.dma_start(k_parts_dram[par].rearrange("s p t -> p s t"), k_parts[:, par, :, :]).then_inc(k_stored, 16)
                if n >= 3:
                    sp.wait_ge(e_full, 8 * (n - 2))
                else:
                    sp.wait_ge(const_ready, 1)
                sp.dma_start(stackK[MASK_ROW:MASK_ROW + 1, buf, :, :],
                             key_mask_dram[r:r + 1, :].rearrange("a (o t) -> a o t", o=1).broadcast_to([1, NH, S]))\
                    .then_inc(stack_loaded[buf], 16)
                sp.wait_ge(q_stored, 16 * (n + 1))
                qv = q_parts_dram[par].rearrange("s (h d) t -> s d h t", d=DH)
                for s, (pq, _) in enumerate(PAIRS):
                    sp.dma_start(stackQ[DH * s:DH * s + DH, buf, :, :], qv[pq]).then_inc(stack_loaded[buf], 16)
                sp.wait_ge(k_stored, 16 * (n + 1))
                kv = k_parts_dram[par].rearrange("s (h d) t -> s d h t", d=DH)
                for s, (_, pk) in enumerate(PAIRS):
                    sp.dma_start(stackK[DH * s:DH * s + DH, buf, :, :], kv[pk]).then_inc(stack_loaded[buf], 16)

            def send_max(n):
                sp.wait_ge(mT_ready, n + 1)
                for part in range(3):
                    sp.dma_start(stackQ[MAX_ROW + part:MAX_ROW + part + 1, n % 3, :, :],
                                 mT[part * NH:(part + 1) * NH, n % 2, :]).then_inc(m_loaded[n % 2], 16)

            def load_expert1(e):
                if e < WRING:
                    sp.wait_ge(e_down, E0)
                else:
                    sp.wait_ge(d_down, 2 * (e - WRING + 1))
                r = e % WRING
                sp.dma_start(w1_b[:, r, :], a["L1_ffn_w1"][e]).then_inc(w1_loaded[r], 16)
                sp.dma_start(w2_b[:, r, :, :], a["L1_ffn_w2"][e].rearrange("(f p) d -> p f d", p=P)).then_inc(w1_loaded[r], 16)

            for lo, hi in SEGMENTS:
                if lo > 0 and last_stage < 3:
                    break
                for i in range(lo - 2, hi):
                    if i + 2 < hi:
                        send_parts(i + 2)
                    if lo <= i + 1 < hi:
                        send_max(i + 1)
                if lo == 0 and last_stage >= 2:
                    first_mixture()
            if last_stage < 2:
                sp.wait_ge(x_ready, SEGMENTS[0][1])
            elif last_stage == 2:
                sp.wait_ge(moe0_ready, B)
            elif last_stage == 3:
                sp.wait_ge(x_ready, NSTEP)
            else:
                for e in range(E1):
                    load_expert1(e)
                sp.wait_ge(final_ready, B)
            sp.dma_start(out.rearrange("b (t p) d -> p (b t) d", p=P), X[:, :, :]).then_inc(out_stored, 16)
            sp.wait_ge(out_stored, 16)

        @block.tensor
        def _(pe):
            def turn_inputs():
                pe.wait_ge(const_ready, 1)
                pe.wait_ge(wr_loaded, 16 * 8)
                for c in range(8):
                    if c >= 2:
                        pe.wait_ge(setup_act, c - 1)
                    pe.transpose(psM[:, c % 2, 0:P], w_rows[:, c, :], ident[:, :]).then_inc(setup_pe, 1)
                pe.wait_ge(ctx_loaded, 16)
                for b in range(B):
                    pe.wait_ge(setup_act, 8 + b - 1)
                    for t in range(QB):
                        mm = pe.transpose(psM[:, b % 2, t * P:(t + 1) * P], ctx_rows[:, QB * b + t, :], ident[:, :])
                    mm.then_inc(setup_pe, 1)
                pe.wait_ge(given_made, 1)
                pe.wait_ge(setup_act, 12)
                for kb in range(QB):
                    for qb in range(QB):
                        mm = pe.transpose(psM[:, kb, 0:P].bitcast(BF16)[:, qb * P:(qb + 1) * P],
                                          given[:, qb, kb * P:(kb + 1) * P], ident_b[:, :])
                mm.then_inc(setup_pe, 1)
                pe.wait_ge(setup_act, 13)

            def turn_x(n):
                if n < B:
                    pe.wait_ge(x_loaded, 16)
                elif n >= SEGMENTS[1][0] and n < SEGMENTS[1][0] + B:
                    pe.wait_ge(moe0_ready, n - SEGMENTS[1][0] + 1)
                else:
                    pe.wait_ge(x_ready, n - B + 1)
                if n - 2 >= lo_of(n):
                    pe.wait_ge(mT_ready, n - 1)
                elif n >= 1:
                    pe.wait_ge(v_ready, n)
                for t in range(QB):
                    mm = pe.transpose(psA[:, t * P:(t + 1) * P], x_in(n // B)[:, QB * (n % B) + t, :], ident[:, :])
                mm.then_inc(t_done, 1)

            def project_q(n):
                if n == 0:
                    pe.wait_ge(w_loaded, 16 * N_W)
                pe.wait_ge(xT_ready, n + 1)
                pe.matmul(psB, Wq[:, n // B, :], xT[:, n % 2, :], start=True, stop=True).then_inc(q_done, 1)

            def source(n):
                return ctxT[:, n % B, :] if CROSS[n // B] else xT[:, n % 2, :]

            def project_k(n):
                pe.wait_ge(q_resid, n + 1)
                pe.matmul(psA, Wk[:, n // B, :], source(n), start=True, stop=True).then_inc(k_done, 1)

            def project_v(n):
                pe.wait_ge(k_resid, n + 1)
                for t in range(QB):
                    mm = pe.matmul(psB[:, t * P:(t + 1) * P], source(n)[:, t * P:(t + 1) * P], Wv[:, n // B, :],
                                   start=True, stop=True)
                mm.then_inc(v_done, 1)

            def score_chunk(n, c):
                layer, buf, qb, kw = n // B, n % 3, c // 8, klen(n // B, c // 8)
                at = m_at["s", n, c]
                if c == 0:
                    pe.wait_ge(stack_loaded[buf], 16 * 13 * (n // 3 + 1))
                if at >= 2:
                    pe.wait_ge(m_used, at - 1)
                kind = KIND[layer]
                for j in range(2):
                    h = 2 * (c % 8) + j
                    dst = psM[:, at % 2, j * S:j * S + kw]
                    mm = pe.matmul(dst, stackQ[0:KEY_ROWS, buf, h, qb * P:(qb + 1) * P],
                                   stackK[0:KEY_ROWS, buf, h, 0:kw], start=True, stop=kind == KEYS)
                    if kind == GIVEN:
                        mm = pe.matmul(dst, ident_b[:, :], given[:, qb, :], start=False, stop=True)
                    if kind in (CAUSAL, WINDOW):
                        far = kind == WINDOW and qb == 1
                        mm = pe.matmul(dst[:, qb * P:(qb + 1) * P], ident_b[:, :], tri[:, 0, :],
                                       start=False, stop=not far)
                        if far:
                            mm = pe.matmul(dst[:, 0:P], ident_b[:, :], tri[:, 1, :], start=False, stop=True)
                mm.then_inc(m_full, 1)

            def exp_chunk(n, c):
                layer, buf, g, kb = n // B, n % 3, c // 2, c % 2
                at, kind = 8 * n + c, KIND[n // B]
                q0 = qlen(layer, kb) * P
                if c == 0:
                    pe.wait_ge(m_loaded[n % 2], 48 * (n // 2 + 1))
                if at >= 2:
                    pe.wait_ge(exp_done, at - 1)
                for j in range(4):
                    h = 4 * g + j
                    dst = psE[:, at % 2, j * S + q0:(j + 1) * S]
                    mm = pe.matmul(dst, stackK[:, buf, h, kb * P:(kb + 1) * P], stackQ[:, buf, h, q0:S],
                                   start=True, stop=kind == KEYS)
                    if kind == GIVEN:
                        mm = pe.matmul(dst, ident_b[:, :], givenT[:, kb, :], start=False, stop=True)
                    if kind in (CAUSAL, WINDOW):
                        far = kind == WINDOW and kb == 0
                        mm = pe.matmul(dst[:, 0:P], ident_b[:, :], tri[:, 1, :], start=False, stop=not far)
                        if far:
                            mm = pe.matmul(dst[:, P:2 * P], ident_b[:, :], tri[:, 0, :], start=False, stop=True)
                mm.then_inc(e_full, 1)

            def values_chunk(n, c):
                g, kb, at = c // 2, c % 2, 8 * n + c
                q0 = qlen(n // B, kb) * P
                if c == 0:
                    pe.wait_ge(v_ready, n + 1)
                if c % 4 == 0 and 2 * n + c // 4 > 0:
                    pe.wait_ge(oT_ready, 2 * n + c // 4)
                pe.wait_ge(exp_done, at + 1)
                for j in range(4):
                    mm = pe.matmul(psO[32 * j:32 * j + 32, g % 2, q0:S], v_aug[:, n % 3, kb, 4 * g + j, :],
                                   probsT[:, at % 3, j, q0:S], start=kb == 0, stop=kb == 1, skip_group_check=True)
                mm.then_inc(pv_done, 1)

            def turn_outputs(n, half):
                at = m_at["o", n, half]
                pe.wait_ge(oT_ready, 2 * n + half + 1)
                if at >= 2:
                    pe.wait_ge(m_used, at - 1)
                for gg in range(2):
                    for qb in range(QB):
                        i = 2 * gg + qb
                        mm = pe.transpose(psM[:, at % 2, i * P:(i + 1) * P], oT[:, half, gg, qb * P:(qb + 1) * P],
                                          ident[:, :])
                mm.then_inc(m_full, 1)

            def turn_normed(n):
                pe.wait_ge(m_used, m_at["o", n, 1] + 1)
                if n + 3 < hi_of(n):
                    pe.wait_ge(v_ready, n + 4)
                else:
                    pe.wait_ge(mT_ready, min(n + 2, hi_of(n)))
                    if n >= 1:
                        pe.wait_ge(wo_read, n)
                for t in range(QB):
                    mm = pe.transpose(psA[:, t * P:(t + 1) * P], o_rows[:, n % 2, t, :], ident[:, :])
                mm.then_inc(nt_done, 1)

            def project_out(n):
                pe.wait_ge(nT_ready, n + 1)
                for t in range(QB):
                    mm = pe.matmul(psB[:, t * P:(t + 1) * P], nT[:, n % 2, t * P:(t + 1) * P], Wo[:, n // B, :],
                                   start=True, stop=True)
                mm.then_inc(wo_done, 1)

            def turn_max(n):
                pe.wait_ge(m_split, n + 1)
                if n - 2 >= lo_of(n):
                    pe.wait_ge(wo_read, n - 1)
                elif n + 1 < hi_of(n):
                    pe.wait_ge(v_ready, n + 2)
                for qb in range(QB):
                    mm = pe.transpose(psA.bitcast(BF16)[0:3 * NH, qb * P:(qb + 1) * P],
                                      m_parts[:, n % 2, qb, :, :].rearrange("p a h -> p (a h)"), ident_b[:, :])
                mm.then_inc(mt_done, 1)

            def lo_of(n):
                return SEGMENTS[0][0] if n < SEGMENTS[0][1] else SEGMENTS[1][0]

            def hi_of(n):
                return SEGMENTS[0][1] if n < SEGMENTS[0][1] else SEGMENTS[1][1]

            def feed_forward():
                pe.wait_ge(x_ready, SEGMENTS[0][1])
                pe.wait_ge(ff_loaded, 16 * (3 + NF))
                for b in range(B + 1):
                    if b < B:
                        if b >= 1:
                            pe.wait_ge(f_xT, b)
                        for t in range(QB):
                            mm = pe.transpose(psA[:, t * P:(t + 1) * P],
                                              XI[:, QB * b + t, :], ident[:, :])
                        mm.then_inc(f_turned, 1)
                        pe.wait_ge(f_xT, b + 1)
                        if b >= 2:
                            pe.wait_ge(f_h, b - 1)
                        for f in range(NF):
                            mm = pe.matmul(psE[:, b % 2, f * S:(f + 1) * S], ff_w1[:, f * P:(f + 1) * P],
                                           xT[:, b % 2, :], start=True, stop=True)
                        mm.then_inc(f_up, 1)
                    if b >= 1:
                        pe.wait_ge(f_h, b)
                        if b >= 3:
                            pe.wait_ge(f_read, b - 2)
                        for t in range(QB):
                            for f in range(NF):
                                mm = pe.matmul(psM[:, (b - 1) % 2, t * P:(t + 1) * P],
                                               ff_h[:, (b - 1) % 2, f, t * P:(t + 1) * P], ff_w2[:, f, :],
                                               start=f == 0, stop=f == NF - 1)
                        mm.then_inc(f_down, 1)

            def turn_all(count):
                for t in range(NT):
                    mm = pe.transpose(psE[:, 0, t * P:(t + 1) * P], X[:, t, :], ident[:, :])
                mm.then_inc(xa_turned, 1)
                pe.wait_ge(xa_ready, count)

            def first_mixture():
                pe.wait_ge(cent_ready, 1)
                pe.transpose(psX[:, 0, 0:G0 + E0], cent_sq[:, :], ident[0:G0 + E0, 0:G0 + E0]).then_inc(cent_turned, 1)
                pe.wait_ge(x3_ready, B)
                turn_all(1)
                pe.wait_ge(centT_ready, 1)
                n = G0 + E0
                for t in range(NT):
                    mm = pe.matmul(psX[:, :, :].rearrange("p a n -> p (a n)")[:, t * n:(t + 1) * n],
                                   xT_all[:, t * P:(t + 1) * P], centT[:, :], start=True, stop=True)
                mm.then_inc(rscore_done, 1)
                for c in range(2):
                    if c == 1:
                        pe.wait_ge(sh_h, 1)
                    for w, half in ((sh_g, 0), (sh_u, 1)):
                        for h in range(2):
                            mm = pe.matmul(psE[:, half, h * 512:(h + 1) * 512], w[:, h * P:(h + 1) * P],
                                           xT_all[:, c * 512:(c + 1) * 512], start=True, stop=True)
                    mm.then_inc(sh_up, 1)
                pe.wait_ge(chosen_ready, 1)
                for t in range(NT):
                    for t2 in range(t + 1):
                        mm = pe.matmul(pos_ps[:, t, :],
                                       before_b[:, :] if t2 == t else ones_b[:, :], chosen[:, t2, :],
                                       start=t2 == 0, stop=t2 == t)
                mm.then_inc(pos_done, 1)
                pe.wait_ge(sh_h, 2)
                for c in range(2):
                    for t in range(4):
                        for h in range(2):
                            mm = pe.matmul(psM[:, c, t * P:(t + 1) * P], sh_hT[:, h, (4 * c + t) * P:(4 * c + t + 1) * P],
                                           sh_d[:, h, :], start=h == 0, stop=h == 1)
                    mm.then_inc(sh_down, 1)
                for j in range(ST // 8):
                    pe.wait_ge(slots_loaded[j], 16)
                    if j >= 2:
                        pe.wait_ge(slotT_ready, j - 1)
                    for t in range(8):
                        mm = pe.transpose(psE[:, j % 2, t * P:(t + 1) * P], slot_rows[:, j % 2, t, :], ident[:, :])
                    mm.then_inc(slots_turned, 1)
                pe.wait_ge(slotT_ready, ST // 8)
                pe.wait_ge(sh_read, 2)
                for e in range(E0 + 1):
                    if e < E0:
                        r, j = e // GRP % WRING, e % GRP
                        if j == 0:
                            pe.wait_ge(we_loaded[r], 48 * (e // GRP // WRING + 1))
                        if e >= 2:
                            pe.wait_ge(e_h, e - 1)
                        for w, at in ((wg_b, 0), (wu_b, 512)):
                            for h in range(2):
                                mm = pe.matmul(psE[:, e % 2, at + h * CAP:at + (h + 1) * CAP],
                                               w[:, r, j, h * P:(h + 1) * P], slotT[:, e * CAP:(e + 1) * CAP],
                                               start=True, stop=True)
                        mm.then_inc(e_up, 1)
                    if e >= 1:
                        d = e - 1
                        r, j = d // GRP % WRING, d % GRP
                        pe.wait_ge(e_h, d + 1)
                        if d >= 2:
                            pe.wait_ge(e_rows, d - 1)
                        for c in range(2):
                            for h in range(2):
                                mm = pe.matmul(psM[0:HC, d % 2, c * P:(c + 1) * P],
                                               hT[:, d % 2, h, c * HC:(c + 1) * HC], wd_b[:, r, j, h, :],
                                               start=h == 0, stop=h == 1)
                        mm.then_inc(e_down, 1)

            def second_mixture():
                pe.wait_ge(m1_loaded, 64)
                pe.wait_ge(x_ready, NSTEP)
                pe.transpose(psX[:, 0, 0:E1 * NF], b1_rows[:, :], ident[0:E1 * NF, 0:E1 * NF]).then_inc(b1_turned, 1)
                turn_all(2)
                pe.wait_ge(b1_ready, 1)
                for t in range(NT):
                    mm = pe.matmul(psX[:, 0, t * E1:(t + 1) * E1], xT_all[:, t * P:(t + 1) * P], router[:, :],
                                   start=True, stop=True)
                mm.then_inc(l_done, 1)
                for n in range(BITS + 1):
                    pe.wait_ge(try_ready, n + 1)
                    pe.matmul(psM[:, n % 2, 0:E1], ones_b[:, :], flag_sum[:, :], start=True, stop=True)\
                        .then_inc(try_counted, 1)
                pe.wait_ge(eq_ready, 1)
                for t in range(NT):
                    for t2 in range(t + 1):
                        mm = pe.matmul(psX[:, 0, t * E1:(t + 1) * E1], before_b[:, :] if t2 == t else ones_b[:, :],
                                       equal[:, t2, :], start=t2 == 0, stop=t2 == t)
                mm.then_inc(eq_ranked, 1)
                pe.wait_ge(w_ready, 1)
                for t in range(NT):
                    mm = pe.transpose(psE[0:E1, 0, t * P:(t + 1) * P], G[:, t, :], ident[:, :])
                mm.then_inc(w_turned, 1)
                pe.wait_ge(wT_ready, 1)
                for c in range(2):
                    for t in range(4):
                        mm = pe.matmul(psM[:, c, t * P:(t + 1) * P], wT[:, (4 * c + t) * P:(4 * c + t + 1) * P],
                                       b2_rows[:, :], start=True, stop=True)
                    mm.then_inc(b2_done, 1)
                for u in range(2 * E1 + 1):
                    if u < 2 * E1:
                        e, c = u // 2, u % 2
                        r = e % WRING
                        if c == 0:
                            pe.wait_ge(w1_loaded[r], 32 * (e // WRING + 1))
                        for f in range(NF):
                            if u >= 1:
                                pe.wait_ge(d_relu, NF * (u - 1) + f + 1)
                            pe.matmul(psE4[:, f, :], w1_b[:, r, f * P:(f + 1) * P], xT_all[:, c * 512:(c + 1) * 512],
                                      start=True, stop=True).then_inc(d_up, 1)
                    if u >= 1:
                        v = u - 1
                        e, c = v // 2, v % 2
                        r = e % WRING
                        pe.wait_ge(d_relu, NF * (v + 1))
                        if v < 2:
                            pe.wait_ge(b2_read, v + 1)
                        else:
                            pe.wait_ge(d_read, v - 1)
                        for t in range(4):
                            for f in range(NF):
                                mm = pe.matmul(psM[:, c, t * P:(t + 1) * P], h1[:, c, f, t * P:(t + 1) * P],
                                               w2_b[:, r, f, :], start=f == 0, stop=f == NF - 1)
                        mm.then_inc(d_down, 1)

            turn_inputs()
            for lo, hi in SEGMENTS:
                if lo > 0 and last_stage < 3:
                    break
                for i in range(lo - 2, hi + 1):
                    early, mid, late, tail = i + 2 < hi, lo <= i + 1 < hi, lo <= i < hi, lo <= i - 1
                    chunk = 0
                    for c in range(8):
                        if c == 0 and early:
                            turn_x(i + 2)
                        if c == 0 and tail:
                            turn_outputs(i - 1, 1)
                        if c == 1 and early:
                            project_q(i + 2)
                        if c == 2 and early:
                            project_k(i + 2)
                        if c == 3 and early:
                            project_v(i + 2)
                        if c == 4 and tail:
                            turn_normed(i - 1)
                        if c == 5 and tail:
                            project_out(i - 1)
                        if c == 6 and late:
                            turn_outputs(i, 0)
                        if c == 7 and mid:
                            turn_max(i + 1)
                        if late:
                            exp_chunk(i, c)
                            if c >= 1:
                                values_chunk(i, c - 1)
                        if mid:
                            for _ in range(SCORES_PER_SLOT[c]):
                                score_chunk(i + 1, chunk)
                                chunk += 1
                    if late:
                        values_chunk(i, 7)
                if lo == 0 and last_stage >= 2:
                    feed_forward()
                    first_mixture()
                if lo > 0 and last_stage >= 4:
                    second_mixture()

        @block.scalar
        def _(act):
            act.wait_ge(setup_pe, 1)
            for c in range(8):
                act.wait_ge(setup_pe, c + 1)
                dst = (Wq, Wk, Wv, Wo)[c % 4][:, 3 + c // 4, :]
                act.activation(dst, psM[:, c % 2, 0:P], ACT.Copy).then_inc(setup_act, 1)
            for b in range(B):
                act.wait_ge(setup_pe, 9 + b)
                act.activation(ctxT[:, b, :], psM[:, b % 2, 0:S], ACT.Copy).then_inc(setup_act, 1)
            act.wait_ge(setup_pe, 13)
            for kb in range(QB):
                mm = act.activation(givenT[:, kb, :], psM[:, kb, 0:P].bitcast(BF16), ACT.Copy)
            mm.then_inc(setup_act, 1)

            def copy_xT(n):
                act.wait_ge(t_done, n + 1)
                if n >= 2:
                    act.wait_ge(v_done, n - 1)
                act.activation(xT[:, n % 2, :], psA, ACT.Copy).then_inc(xT_ready, 1)

            def high_part(n, done, parts, ps, bias, stored, ready):
                act.wait_ge(done, n + 1)
                if n >= 2:
                    act.wait_ge(stored, 16 * (n - 1))
                if n // B == 0:
                    mm = act.activation(parts[:, n % 2, 0, :], ps, ACT.Copy)
                else:
                    mm = act.activation(parts[:, n % 2, 0, :], ps, ACT.Identity, bias=bias)
                mm.then_inc(ready, 1)

            def exp_chunk(n, c):
                at, q0 = 8 * n + c, qlen(n // B, c % 2) * P
                act.wait_ge(e_full, at + 1)
                if at >= 3:
                    act.wait_ge(pv_done, at - 2)
                act.activation(probsT[:, at % 3, :, q0:S],
                               psE[:, at % 2, :].rearrange("p (h q) -> p h q", h=4)[:, :, q0:S],
                               ACT.Exp, scale=SCALE).then_inc(exp_done, 1)

            def copy_outputs(n, half):
                act.wait_ge(pv_done, 8 * n + 4 * half + 4)
                if n >= 1:
                    act.wait_ge(m_full, m_at["o", n - 1, half] + 1)
                act.activation(oT[:, half, :, :], psO[:, :, :], ACT.Copy).then_inc(oT_ready, 1)

            def copy_normed(n):
                act.wait_ge(nt_done, n + 1)
                act.activation(nT[:, n % 2, :], psA, ACT.Copy).then_inc(nT_ready, 1)

            def copy_max(n):
                act.wait_ge(mt_done, n + 1)
                if n >= 2:
                    act.wait_ge(m_loaded[n % 2], 48 * (n // 2))
                act.activation(mT[:, n % 2, :], psA.bitcast(BF16)[0:3 * NH, 0:S], ACT.Copy).then_inc(mT_ready, 1)

            def feed_forward():
                act.wait_ge(ff_loaded, 16 * (3 + NF))
                for b in range(B):
                    act.wait_ge(f_turned, b + 1)
                    if b >= 2:
                        act.wait_ge(f_up, b - 1)
                    act.activation(xT[:, b % 2, :], psA, ACT.Copy).then_inc(f_xT, 1)
                    act.wait_ge(f_up, b + 1)
                    if b >= 2:
                        act.wait_ge(f_down, b - 1)
                    for f in range(NF):
                        mm = act.activation(ff_h[:, b % 2, f, :], psE[:, b % 2, f * S:(f + 1) * S], ACT.Relu,
                                            bias=ff_b1[:, f:f + 1])
                    mm.then_inc(f_h, 1)

            def first_mixture():
                act.wait_ge(cent_turned, 1)
                act.activation(centT[:, :], psX[:, 0, 0:G0 + E0], ACT.Copy).then_inc(centT_ready, 1)
                act.wait_ge(xa_turned, 1)
                act.activation(xT_all[:, :], psE[:, 0, :], ACT.Copy).then_inc(xa_ready, 1)
                act.wait_ge(gate_in, 1)
                act.activation(gate[:, :, :], gate[:, :, :], ACT.Exp).then_inc(gate_exp, 1)
                for c in range(2):
                    act.wait_ge(sh_up, c + 1)
                    act.activation(silu_sh[:, c, :, :].rearrange("p h n -> p (h n)"), psE[:, 0, :], ACT.Silu)\
                        .then_inc(sh_silu, 1)
                for j in range(ST // 8):
                    if j == 0:
                        act.wait_ge(sh_down, 2)
                    act.wait_ge(slots_turned, j + 1)
                    act.activation(slotT[:, 8 * j * P:8 * (j + 1) * P], psE[:, j % 2, :], ACT.Copy).then_inc(slotT_ready, 1)
                for e in range(E0 + 1):
                    if e < E0:
                        act.wait_ge(e_up, e + 1)
                        if e >= 2:
                            act.wait_ge(e_h, e - 1)
                        act.activation(silu_e[:, e % 2, :], psE[:, e % 2, 0:2 * CAP], ACT.Silu).then_inc(e_silu, 1)
                    if e >= 1:
                        d = e - 1
                        act.wait_ge(e_down, d + 1)
                        if d >= 2:
                            act.wait_ge(y_stored[d % 2], 16 * (d // 2))
                        act.activation(y_rows[:, d % 2, :, :], psM[0:HC, d % 2, 0:2 * D].rearrange("p (c d) -> p c d", c=2),
                                       ACT.Copy).then_inc(e_rows, 1)

            def second_mixture():
                act.wait_ge(b1_turned, 1)
                act.activation(b1_cols[:, :], psX[:, 0, 0:E1 * NF], ACT.Copy).then_inc(b1_ready, 1)
                act.wait_ge(xa_turned, 2)
                act.activation(xT_all[:, :], psE[:, 0, :], ACT.Copy).then_inc(xa_ready, 1)
                act.wait_ge(l_exp_in, 1)
                act.activation(G[:, :, :], G[:, :, :], ACT.Exp).then_inc(l_exp, 1)
                act.wait_ge(w_turned, 1)
                act.activation(wT[:, :], psE[0:E1, 0, :], ACT.Copy).then_inc(wT_ready, 1)
                for u in range(2 * E1):
                    if u >= 2:
                        act.wait_ge(d_down, u - 1)
                    for f in range(NF):
                        act.wait_ge(d_up, NF * u + f + 1)
                        j = u // 2 * NF + f
                        act.activation(h1[:, u % 2, f, :], psE4[:, f, :], ACT.Relu, bias=b1_cols[:, j:j + 1])\
                            .then_inc(d_relu, 1)

            for lo, hi in SEGMENTS:
                if lo > 0 and last_stage < 3:
                    break
                for i in range(lo - 2, hi + 1):
                    early, mid, late, tail = i + 2 < hi, lo <= i + 1 < hi, lo <= i < hi, lo <= i - 1
                    for c in range(8):
                        if c == 0 and early:
                            copy_xT(i + 2)
                        if c == 1 and early:
                            n = i + 2
                            if n == 0:
                                act.wait_ge(w_loaded, 16 * N_W)
                            high_part(n, q_done, q_parts, psB, bqk[:, n // B, 0:1], q_stored, q_hi)
                        if c == 2 and early:
                            high_part(n, k_done, k_parts, psA, bqk[:, n // B, 1:2], k_stored, k_hi)
                        if c == 4 and tail:
                            copy_normed(i - 1)
                        if c == 5 and late:
                            copy_outputs(i, 0)
                        if c == 7 and mid:
                            copy_max(i + 1)
                        if late:
                            exp_chunk(i, c)
                    if late:
                        copy_outputs(i, 1)
                if lo == 0 and last_stage >= 2:
                    feed_forward()
                    first_mixture()
                if lo > 0 and last_stage >= 4:
                    second_mixture()

        @block.vector
        def _(dve):
            chain = [0]

            def link(ins):
                chain[0] += 1
                ins.then_inc(dve_chain, 1)
                dve.wait_ge(dve_chain, chain[0])

            def rest(n, hi_ready, parts, restof, ps, bias, ready):
                dve.wait_ge(hi_ready, n + 1)
                if n >= 2:
                    dve.wait_ge({id(q_rest): q_split, id(k_rest): k_split}[id(restof)], n - 1)
                if n // B == 0:
                    dve.tensor_tensor(restof[:, n % 2, :], ps, parts[:, n % 2, 0, :], ALU.subtract).then_inc(ready, 1)
                else:
                    dve.scalar_tensor_tensor(restof[:, n % 2, :], ps, bias, parts[:, n % 2, 0, :],
                                             ALU.add, ALU.subtract).then_inc(ready, 1)

            def take_v(n):
                dve.wait_ge(v_done, n + 1)
                if n >= 3:
                    dve.wait_ge(pv_done, 8 * (n - 2))
                dst = v_aug[:, n % 3, :, :, 0:DH]
                src = psB.rearrange("p (t h d) -> p t h d", t=QB, d=DH)
                if n // B == 0:
                    dve.tensor_copy(dst, src).then_inc(v_ready, 1)
                else:
                    bias = bvo[:, n // B, 0, :].rearrange("p (o h d) -> p o h d", o=1, d=DH).broadcast_to([P, QB, NH, DH])
                    dve.tensor_tensor(dst, src, bias, ALU.add).then_inc(v_ready, 1)

            def row_max(n, c):
                at, qb, kw = m_at["s", n, c], c // 8, klen(n // B, c // 8)
                dve.wait_ge(m_full, at + 1)
                if c == 0 and n >= 1:
                    dve.wait_ge(m_split, n)
                h = 2 * (c % 8)
                mm = dve.tensor_reduce(mx[:, qb, h:h + 2],
                                       psM[:, at % 2, :].rearrange("p (h k) -> p h k", h=2)[:, :, 0:kw],
                                       AX, ALU.max)
                mm.then_inc(m_used, 1)

            def norm_outputs(n, half):
                at = m_at["o", n, half]
                ps = psM[:, at % 2, :].rearrange("p (g q h e) -> p q g h e", g=2, q=QB, h=4)
                dve.wait_ge(m_full, at + 1)
                if n >= 2:
                    dve.wait_ge(nt_done, n - 1)
                for qb in range(QB):
                    mm = dve.reciprocal(inv_den[:, half, qb, :].rearrange("p (g h) -> p g h", g=2),
                                        ps[:, qb, :, :, DH])
                link(mm)
                for qb in range(QB):
                    dst = o_rows[:, n % 2, qb, half * 64:half * 64 + 64].rearrange("p (g h d) -> p g h d", g=2, h=4)
                    inv = inv_den[:, half, qb, :].rearrange("p (g h o) -> p g h o", g=2, o=1)\
                        .broadcast_to([P, 2, 4, DH])
                    mm = dve.tensor_tensor(dst, ps[:, qb, :, :, 0:DH], inv, ALU.mult)
                mm.then_inc(m_used, 1)

            def layer_norm(src, dst, par, gain=None):
                for t in range(QB):
                    mm = dve.bn_stats(stats[:, par, t, :], src[:, t, :])
                link(mm)
                for t in range(QB):
                    mm = dve.bn_aggr(mv[:, par, t, :], stats[:, par, t, :])
                link(mm)
                dve.tensor_scalar(var_eps[:, par, :], mv[:, par, :, 1], EPS, None, ALU.add).then_inc(var_ready, 1)
                norms[0] += 1
                dve.wait_ge(rstd_ready, norms[0])
                for t in range(QB):
                    mm = dve.tensor_scalar(dst[:, t, :], src[:, t, :], mv[:, par, t, 0:1], rstd[:, par, t:t + 1],
                                           ALU.subtract, ALU.mult)
                if gain is not None:
                    gb = [ln_gb[:, gain, c, :].rearrange("p (o d) -> p o d", o=1).broadcast_to([P, QB, D])
                          for c in range(2)]
                    link(mm)
                    link(dve.tensor_tensor(dst, dst, gb[0], ALU.mult))
                    mm = dve.tensor_tensor(dst, dst, gb[1], ALU.add)
                return mm

            norms = [0]

            def finish(n):
                layer, par, b = n // B, n % 2, n % B
                dve.wait_ge(wo_done, n + 1)
                xb, dst = x_in(layer)[:, QB * b:QB * (b + 1), :], x_out(layer)[:, QB * b:QB * (b + 1), :]
                bias = bvo[:, layer, 1, :].rearrange("p (o d) -> p o d", o=1).broadcast_to([P, QB, D])
                dve.tensor_tensor(res[:, par, :, :], psB.rearrange("p (t d) -> p t d", t=QB), bias, ALU.add)\
                    .then_inc(wo_read, 1)
                dve.wait_ge(wo_read, n + 1)
                link(dve.tensor_tensor(res[:, par, :, :], res[:, par, :, :], xb, ALU.add))
                layer_norm(res[:, par], dst, par, AFFINE.get(layer)).then_inc(x_ready, 1)

            def spread(v, shape):
                return v.broadcast_to(shape)

            def feed_forward():
                for b in range(B):
                    par = b % 2
                    xb, xi = X[:, QB * b:QB * (b + 1), :], XI[:, QB * b:QB * (b + 1), :]
                    r = res[:, par, :, :]
                    dve.wait_ge(f_down, b + 1)
                    bias = ff_b2[:, :].rearrange("p (o d) -> p o d", o=1).broadcast_to([P, QB, D])
                    dve.tensor_tensor(r, psM[:, par, 0:QB * D].rearrange("p (t d) -> p t d", t=QB), bias, ALU.add)\
                        .then_inc(f_read, 1)
                    dve.wait_ge(f_read, b + 1)
                    link(dve.tensor_tensor(r, r, xi, ALU.add))
                    link(layer_norm(r, r, par, 2))
                    link(dve.tensor_tensor(r, r, xb, ALU.add))
                    layer_norm(r, xb, par).then_inc(x3_ready, 1)

            def first_mixture():
                n = G0 + E0
                dve.wait_ge(r_loaded, 16 * 6)
                link(dve.tensor_tensor(cent_sq[:, :], cent[:, :], cent[:, :], ALU.mult))
                link(dve.tensor_reduce(cent_n[:, 0:1], cent_sq[:, :], AX, ALU.add))
                dve.tensor_scalar(cent_n[:, 0:1], cent_n[:, 0:1], 1e-24, None, ALU.max).then_inc(pow_in, 1)
                dve.wait_ge(pow_out, 1)
                dve.tensor_scalar(cent_sq[:, :], cent[:, :], cent_n[:, 1:2], None, ALU.mult).then_inc(cent_ready, 1)
                link(dve.tensor_tensor(sq[:, :, :], X[:, :, :], X[:, :, :], ALU.mult))
                link(dve.tensor_reduce(norm_x[:, 0, :], sq[:, :, :], AX, ALU.add))
                dve.tensor_scalar(norm_x[:, 0, :], norm_x[:, 0, :], 1e-24, None, ALU.max).then_inc(pow_in, 1)
                dve.wait_ge(pow_out, 2)
                dve.wait_ge(rscore_done, 1)
                link(dve.tensor_tensor(scs[:, :, :], rs_ps, norm_x[:, 1, :].rearrange("p (t o) -> p t o", o=1)
                                       .broadcast_to([P, NT, n]), ALU.mult))
                gs = scs[:, :, 0:G0]
                gj = gs.rearrange("p t (o j) -> p t o j", o=1).broadcast_to([P, NT, G0, G0])
                gi = gs.rearrange("p t (i o) -> p t i o", o=1).broadcast_to([P, NT, G0, G0])
                dve.tensor_tensor(g_gt[:, :, :, :], gj, gi, ALU.is_gt)
                link(dve.tensor_tensor(g_eq[:, :, :, :], gj, gi, ALU.is_equal))
                low = lower[:, :, :].rearrange("p (o i) j -> p o i j", o=1).broadcast_to([P, NT, G0, G0])
                link(dve.tensor_tensor(g_eq[:, :, :, :], g_eq[:, :, :, :], low, ALU.mult))
                link(dve.tensor_tensor(g_gt[:, :, :, :], g_gt[:, :, :, :], g_eq[:, :, :, :], ALU.add))
                link(dve.tensor_reduce(g_rank[:, :, :], g_gt[:, :, :, :], AX, ALU.add))
                link(dve.tensor_scalar(g_in[:, :, :], g_rank[:, :, :], float(max(1, G0 // 2)), None, ALU.is_lt))
                dve.tensor_scalar(g_pen[:, :, :], g_in[:, :, :], 1e9, -1e9, ALU.mult, ALU.add)
                es = scs[:, :, G0:n]
                link(dve.tensor_tensor(es, es, bias0[:, :].rearrange("p (o e) -> p o e", o=1)
                                       .broadcast_to([P, NT, E0]), ALU.add))
                es4 = es.rearrange("p t (g c) -> p t g c", g=G0)
                sp4 = [NT, G0, E0 // G0]
                link(dve.tensor_tensor(es4, es4, g_in[:, :, :].rearrange("p t (g o) -> p t g o", o=1)
                                       .broadcast_to([P] + sp4), ALU.mult))
                link(dve.tensor_tensor(es4, es4, g_pen[:, :, :].rearrange("p t (g o) -> p t g o", o=1)
                                       .broadcast_to([P] + sp4), ALU.add))
                for t in range(NT):
                    mm = dve.max(top_v[:, t, :], scs[:, t, G0:n])
                link(mm)
                for t in range(NT):
                    mm = dve.max_index(top_i[:, t, :], top_v[:, t, :], scs[:, t, G0:n])
                link(mm)
                tv = top_v[:, :, 0:K0]
                dve.tensor_tensor(gate[:, :, :], tv, top_v[:, :, 0:1].broadcast_to([P, NT, K0]), ALU.subtract)\
                    .then_inc(gate_in, 1)
                link(dve.tensor_copy(top_f[:, :, :], top_i[:, :, 0:K0]))
                tf = top_f[:, :, :].rearrange("p t k -> p (t k)")
                NK = NT * K0
                link(dve.tensor_tensor(hot[:, :, :], iota_e[:, :].rearrange("p (o e) -> p o e", o=1)
                                       .broadcast_to([P, NK, E0]),
                                       tf.rearrange("p (k o) -> p k o", o=1).broadcast_to([P, NK, E0]), ALU.is_equal))
                hv = hot[:, :, :].rearrange("p (t k) e -> p t k e", k=K0)
                ch = hot_pos[:, 0:3 * NT, :].rearrange("p (c t) e -> p c t e", c=3)
                dve.tensor_tensor(ch[:, 0], hv[:, :, 0, :], hv[:, :, 1, :], ALU.add)
                link(dve.tensor_tensor(ch[:, 1], hv[:, :, 2, :], hv[:, :, 3, :], ALU.add))
                dve.tensor_tensor(chosen[:, :, :], ch[:, 0], ch[:, 1], ALU.add).then_inc(chosen_ready, 1)
                dve.wait_ge(chosen_ready, 1)
                dve.wait_ge(gate_exp, 1)
                link(dve.tensor_reduce(gate_sum[:, 0, :], gate[:, :, :], AX, ALU.add))
                link(dve.reciprocal(gate_sum[:, 1, :], gate_sum[:, 0, :]))
                link(dve.tensor_tensor(gate[:, :, :], gate[:, :, :], gate_sum[:, 1, :].rearrange("p (t o) -> p t o", o=1)
                                       .broadcast_to([P, NT, K0]), ALU.mult))
                shared_h(0)
                dve.wait_ge(pos_done, 1)
                pv4 = pos_ps.rearrange("p t (o e) -> p t o e", o=1).broadcast_to([P, NT, K0, E0])
                link(dve.tensor_tensor(hot_pos[:, :, :].rearrange("p (t k) e -> p t k e", k=K0), hv, pv4, ALU.mult))
                link(dve.tensor_reduce(pos[:, :], hot_pos[:, :, :], AX, ALU.add))
                dve.tensor_scalar(over[:, :], pos[:, :], float(CAP), None, ALU.is_ge)
                dve.tensor_scalar(slot[:, 0, :], pos[:, :], float(CAP - 1), None, ALU.min)
                link(dve.tensor_scalar(slot[:, 1, :], tf, float(CAP), None, ALU.mult))
                dve.tensor_tensor(slot[:, 0, :], slot[:, 0, :], slot[:, 1, :], ALU.add)
                link(dve.tensor_tensor(slot[:, 1, :], slot[:, 1, :], pos[:, :], ALU.add))
                link(dve.scalar_tensor_tensor(slot[:, 2, :], over[:, :], FAR, slot[:, 1, :], ALU.mult, ALU.add))
                dve.tensor_copy(slot_to[:, :], slot[:, 2, :])
                dve.tensor_copy(slot_from[:, :], slot[:, 0, :]).then_inc(slots_ready, 1)
                link(dve.tensor_scalar(over[:, :], over[:, :], -1.0, 1.0, ALU.mult, ALU.add))
                gf = gate[:, :, :].rearrange("p t k -> p (t k)")
                link(dve.tensor_tensor(gf, gf, over[:, :], ALU.mult))
                shared_h(1)
                for c in range(2):
                    dve.wait_ge(sh_down, c + 1)
                    dve.tensor_copy(Y[:, 4 * c:4 * c + 4, :], psM[:, c, :].rearrange("p (t d) -> p t d", t=4))\
                        .then_inc(sh_read, 1)
                for e in range(E0):
                    dve.wait_ge(e_silu, e + 1)
                    if e >= 2:
                        dve.wait_ge(e_down, e - 1)
                    dve.tensor_tensor(hT[:, e % 2, :, :].rearrange("p h c -> p (h c)"), silu_e[:, e % 2, :],
                                      psE[:, e % 2, 512:512 + 2 * CAP], ALU.mult).then_inc(e_h, 1)
                dve.wait_ge(sh_read, 2)
                for k in range(K0):
                    for t in range(NT):
                        if k == 0:
                            dve.wait_ge(gathered[t], 16 * K0)
                        mm = dve.scalar_tensor_tensor(Y[:, t, :], y_chosen[:, t * K0 + k, :], gate[:, t, k:k + 1],
                                                      Y[:, t, :], ALU.mult, ALU.add)
                    link(mm)
                link(dve.tensor_tensor(Y[:, :, :], Y[:, :, :], X[:, :, :], ALU.add))
                for b in range(B):
                    layer_norm(Y[:, QB * b:QB * (b + 1), :], X[:, QB * b:QB * (b + 1), :], b % 2).then_inc(moe0_ready, 1)

            def second_mixture():
                dve.wait_ge(m1_loaded, 64)
                dve.wait_ge(l_done, 1)
                one = lambda v: v.rearrange("p (t o) -> p t o", o=1).broadcast_to([P, NT, E1])
                every = lambda v: v.rearrange("p (o e) -> p o e", o=1).broadcast_to([P, NT, E1])
                link(dve.tensor_tensor(G[:, :, :], psX[:, 0, 0:NT * E1].rearrange("p (t e) -> p t e", t=NT),
                                       every(router_bias[:, :]), ALU.add))
                link(dve.tensor_reduce(g_top[:, :], G[:, :, :], AX, ALU.max))
                dve.tensor_tensor(G[:, :, :], G[:, :, :], one(g_top[:, :]), ALU.subtract).then_inc(l_exp_in, 1)
                dve.memset(low_cut[:, :], 0.0)
                link(dve.memset(try_cut[:, :].bitcast(I32), 1 << (BITS - 1)))
                dve.wait_ge(l_exp, 1)
                link(dve.tensor_reduce(g_top[:, :], G[:, :, :], AX, ALU.add))
                link(dve.reciprocal(g_top[:, :], g_top[:, :]))
                link(dve.tensor_tensor(G[:, :, :], G[:, :, :], one(g_top[:, :]), ALU.mult))

                def count(flags, n):
                    with nc.allow_low_precision(reason="sums up to 8 of zeros and ones"):
                        dve.tensor_reduce(flag_sum[:, :], flags.rearrange("p t e -> p e t"), AX, ALU.add)\
                            .then_inc(try_ready, 1)
                    dve.wait_ge(try_counted, n + 1)

                for n in range(BITS):
                    link(dve.tensor_tensor(flag[:, 0, :, :], G[:, :, :], every(try_cut[:, :]), ALU.is_ge))
                    count(flag[:, 0, :, :], n)
                    link(dve.scalar_tensor_tensor(try_ok[:, :], psM[:, n % 2, 0:E1], K1 - 0.5, try_cut[:, :],
                                                  ALU.is_gt, ALU.mult))
                    link(dve.tensor_tensor(low_cut[:, :], low_cut[:, :], try_ok[:, :], ALU.max))
                    if n < BITS - 1:
                        link(dve.tensor_scalar(try_cut[:, :].bitcast(I32), low_cut[:, :].bitcast(I32),
                                               1 << (BITS - 2 - n), None, ALU.bitwise_or))
                dve.tensor_tensor(equal[:, :, :], G[:, :, :], every(low_cut[:, :]), ALU.is_equal).then_inc(eq_ready, 1)
                link(dve.tensor_tensor(flag[:, 0, :, :], G[:, :, :], every(low_cut[:, :]), ALU.is_gt))
                count(flag[:, 0, :, :], BITS)
                link(dve.tensor_scalar(try_ok[:, :], psM[:, BITS % 2, 0:E1], -1.0, float(K1), ALU.mult, ALU.add))
                dve.wait_ge(eq_ranked, 1)
                link(dve.tensor_tensor(flag[:, 1, :, :], psX[:, 0, 0:NT * E1].rearrange("p (t e) -> p t e", t=NT),
                                       every(try_ok[:, :]), ALU.is_lt))
                link(dve.tensor_tensor(flag[:, 1, :, :], flag[:, 1, :, :], equal[:, :, :], ALU.mult))
                link(dve.tensor_tensor(flag[:, 0, :, :], flag[:, 0, :, :], flag[:, 1, :, :], ALU.add))
                dve.tensor_tensor(G[:, :, :], G[:, :, :], flag[:, 0, :, :], ALU.mult).then_inc(w_ready, 1)
                dve.wait_ge(w_ready, 1)
                for c in range(2):
                    dve.wait_ge(b2_done, c + 1)
                    dve.tensor_copy(Y[:, 4 * c:4 * c + 4, :], psM[:, c, :].rearrange("p (t d) -> p t d", t=4))\
                        .then_inc(b2_read, 1)
                dve.wait_ge(b2_read, 2)
                for u in range(2 * E1):
                    e, c = u // 2, u % 2
                    dve.wait_ge(d_down, u + 1)
                    if u >= 2:
                        dve.wait_ge(d_read, u - 1)
                    for t in range(4):
                        mm = dve.scalar_tensor_tensor(Y[:, 4 * c + t, :], psM[:, c, t * P:(t + 1) * P],
                                                      G[:, 4 * c + t, e:e + 1], Y[:, 4 * c + t, :], ALU.mult, ALU.add)
                    mm.then_inc(d_read, 1)
                dve.wait_ge(d_read, 2 * E1)
                link(dve.tensor_tensor(Y[:, :, :], Y[:, :, :], X[:, :, :], ALU.add))
                for b in range(B):
                    layer_norm(Y[:, QB * b:QB * (b + 1), :], X[:, QB * b:QB * (b + 1), :], b % 2).then_inc(final_ready, 1)

            def shared_h(c):
                dve.wait_ge(sh_silu, c + 1)
                dve.tensor_tensor(sh_hT[:, :, c * 512:(c + 1) * 512], silu_sh[:, c, :, :],
                                  psE[:, 1, :].rearrange("p (h n) -> p h n", h=2), ALU.mult).then_inc(sh_h, 1)

            dve.memset(slot_rows[:, :, :, :], 0.0).then_inc(zero_ready, 1)
            dve.wait_ge(mask_loaded, 32)
            dve.wait_ge(const_ready, 1)
            dve.tensor_scalar(given[:, :, :], given_i[:, :, :], 0.0, MASKED, ALU.is_equal, ALU.mult).then_inc(given_made, 1)
            dve.tensor_scalar(keys_row[0:B, :], keys_i[:, :], 0.0, MASKED, ALU.is_equal, ALU.mult).then_inc(keys_made, 1)
            dve.wait_ge(w_loaded, 16 * N_W)
            for lo, hi in SEGMENTS:
                if lo > 0 and last_stage < 3:
                    break
                for i in range(lo - 2, hi + 1):
                    early, mid, late, tail = i + 2 < hi, lo <= i + 1 < hi, lo <= i < hi, lo <= i - 1
                    chunk = 0
                    for c in range(8):
                        n = i + 2
                        if c == 0 and tail:
                            norm_outputs(i - 1, 1)
                        if c == 1 and early:
                            rest(n, q_hi, q_parts, q_rest, psB, bqk[:, n // B, 0:1], q_resid)
                        if c == 2 and early:
                            rest(n, k_hi, k_parts, k_rest, psA, bqk[:, n // B, 1:2], k_resid)
                        if c == 3 and early:
                            take_v(n)
                        if c == 6 and tail:
                            finish(i - 1)
                        if c == 6 and late:
                            norm_outputs(i, 0)
                        if mid:
                            for _ in range(SCORES_PER_SLOT[c]):
                                row_max(i + 1, chunk)
                                chunk += 1
                if lo == 0 and last_stage >= 2:
                    feed_forward()
                    first_mixture()
                if lo > 0 and last_stage >= 4:
                    second_mixture()

        @block.gpsimd
        def _(pool):
            chain = [0]

            def link(ins):
                chain[0] += 1
                ins.then_inc(pool_chain, 1)
                pool.wait_ge(pool_chain, chain[0])

            pool.dma_start(given_i[:, :, :], a["mask_1x1xSxS2_ik0"].rearrange("a c (t p) k -> p (a c t) k", p=P))\
                .then_inc(mask_loaded, 16)
            pool.dma_start(keys_i[:, :], a["mask_Bx1x1xS2_if1"].rearrange("b x y k -> b (x y k)")).then_inc(mask_loaded, 16)
            for t in (ident, ident_b, tri, v_aug, keys_row, stackQ, stackK):
                link(pool.memset(t[tuple(slice(None) for _ in t.shape)], 0.0))
            link(pool.memset(neg_half[:, :], -0.5))
            for t in (ident, ident_b):
                link(pool.affine_select(out=t[:, :], in_=t[:, :], compare_op=ALU.not_equal, fill=1.0, base=0,
                                   pattern=[[-1, P]], channel_multiplier=1))
            link(pool.affine_select(out=tri[:, 0, :], in_=tri[:, 0, :], compare_op=ALU.is_ge, fill=MASKED, base=0,
                               pattern=[[-1, P]], channel_multiplier=1))
            link(pool.affine_select(out=tri[:, 1, :], in_=tri[:, 1, :], compare_op=ALU.is_ge, fill=MASKED, base=0,
                               pattern=[[1, P]], channel_multiplier=-1))
            for buf in range(3):
                v = stackQ[32:64, buf, :, :].rearrange("p h t -> p (h t)")
                link(pool.affine_select(out=v, in_=v, compare_op=ALU.not_equal, fill=1.0, base=32 - MASK_ROW,
                                   pattern=[[0, NH * S]], channel_multiplier=1))
                v = stackK[64:ALL_ROWS, buf, :, :].rearrange("p h t -> p (h t)")
                link(pool.affine_select(out=v, in_=v, compare_op=ALU.is_ge, fill=1.0, base=MAX_ROW - 1 - 64,
                                   pattern=[[0, NH * S]], channel_multiplier=-1))
            link(pool.memset(ones_b[:, :], 1.0))
            link(pool.affine_select(out=before_b[:, :], in_=ones_b[:, :], compare_op=ALU.is_gt, fill=0.0, base=0,
                                    pattern=[[1, P]], channel_multiplier=-1))
            link(pool.memset(lower[:, :, :], 1.0))
            link(pool.affine_select(out=lower[:, :, :], in_=lower[:, :, :], compare_op=ALU.is_gt, fill=0.0, base=0,
                                    pattern=[[1, G0], [-1, G0]], channel_multiplier=0))
            link(pool.iota(iota_e[:, :], pattern=[[1, E0]], base=0, channel_multiplier=0,
                           allow_small_or_imprecise_dtypes=True))
            mm = pool.memset(v_aug[:, :, :, :, DH:DH + 1], 1.0)
            mm.then_inc(const_ready, 1)

            def split(n, resid, restof, parts, ready):
                pool.wait_ge(resid, n + 1)
                link(pool.tensor_copy(parts[:, n % 2, 1, :], restof[:, n % 2, :]))
                pool.tensor_tensor(parts[:, n % 2, 2, :], restof[:, n % 2, :], parts[:, n % 2, 1, :],
                                   ALU.subtract).then_inc(ready, 1)

            def split_max(n):
                par = n % 2
                pool.wait_ge(m_used, m_at["s", n, 15] + 1)
                if n >= 2:
                    pool.wait_ge(mt_done, n - 1)
                part = [m_parts[:, par, :, c, :] for c in range(3)]
                r = m_rest[:, par, :, :]
                link(pool.tensor_scalar(r, mx[:, :, :], -1.0, None, ALU.mult))
                link(pool.tensor_copy(part[0], r))
                link(pool.tensor_tensor(r, r, part[0], ALU.subtract))
                link(pool.tensor_copy(part[1], r))
                pool.tensor_tensor(part[2], r, part[1], ALU.subtract).then_inc(m_split, 1)

            def root(par):
                norms[0] += 1
                pool.wait_ge(var_ready, norms[0])
                pool.tensor_tensor(rstd[:, par, :], var_eps[:, par, :], neg_half[:, 0:QB], ALU.pow).then_inc(rstd_ready, 1)

            def first_mixture():
                pool.wait_ge(pow_in, 1)
                pool.tensor_tensor(cent_n[:, 1:2], cent_n[:, 0:1], neg_half[0:G0 + E0, 0:1], ALU.pow).then_inc(pow_out, 1)
                pool.wait_ge(pow_in, 2)
                pool.tensor_tensor(norm_x[:, 1, :], norm_x[:, 0, :], neg_half[:, :], ALU.pow).then_inc(pow_out, 1)
                pool.wait_ge(slots_ready, 1)
                pool.wait_ge(zero_stored, 16 * (ST // 8))
                for t in range(NT):
                    for k in range(K0):
                        j = t * K0 + k
                        pool.indirect_dma_start(
                            out=slot_x_dram, out_offset=bass.IndirectOffsetOnAxis(ap=slot_to[:, j:j + 1], axis=0),
                            in_=X[:, t, :], in_offset=None, bounds_check=SLOTS - 1, oob_is_err=False)\
                            .then_inc(scattered, 16)
                for j in range(2):
                    pool.wait_ge(y_stored[j], 16 * (E0 // 2))
                pool.wait_ge(e_up, E0)
                for t in range(NT):
                    for k in range(K0):
                        j = t * K0 + k
                        pool.indirect_dma_start(
                            out=y_chosen[:, j, :], out_offset=None, in_=slot_y_dram,
                            in_offset=bass.IndirectOffsetOnAxis(ap=slot_from[:, j:j + 1], axis=0),
                            bounds_check=SLOTS - 1, oob_is_err=False).then_inc(gathered[t], 16)
                for b in range(B):
                    root(b % 2)

            norms = [0]
            for lo, hi in SEGMENTS:
                if lo > 0 and last_stage < 3:
                    break
                for i in range(lo - 2, hi + 1):
                    if i + 2 < hi:
                        split(i + 2, q_resid, q_rest, q_parts, q_split)
                        split(i + 2, k_resid, k_rest, k_parts, k_split)
                    if lo <= i + 1 < hi:
                        split_max(i + 1)
                    if lo <= i - 1:
                        root((i - 1) % 2)
                if lo == 0 and last_stage >= 2:
                    for b in range(B):
                        root(b % 2)
                        root(b % 2)
                    first_mixture()
                if lo > 0 and last_stage >= 4:
                    for b in range(B):
                        root(b % 2)


def kernel(**inputs):
    import numpy as _np
    import concourse.bacc as _bacc
    from concourse import mybir as _mybir
    from concourse.bass_utils import run_bass_kernel_spmd as _run

    nc = _bacc.Bacc("TRN2", target_bir_lowering=False, num_devices=1)
    arrays, args = {}, {}
    for name, value in inputs.items():
        v = _np.ascontiguousarray(value)
        arrays[f"in_{name}"] = v
        args[name] = nc.dram_tensor(f"in_{name}", v.shape, _mybir.dt.from_np(v.dtype), kind="ExternalInput").ap()
    out = nc.dram_tensor("out", (B, S, D), F32, kind="ExternalOutput").ap()
    build(nc, args, out)
    r = _run(nc, [arrays], core_ids=[0])
    return r.results[0]["out"]
```

```python
from contextlib import ExitStack

import concourse.bass as bass
from concourse import mybir

ALU = mybir.AluOpType
ACT = mybir.ActivationFunctionType
AX = mybir.AxisListType.X
F32 = mybir.dt.float32
BF16 = mybir.dt.bfloat16
I32 = mybir.dt.int32
U32 = mybir.dt.uint32

P = 128
B, S, D = 4, 256, 128
NT = B * S // P
NH, DH = 16, 8
QB = S // P
SCALE = float(DH) ** -0.5
EPS = 1e-5
MASKED = -(2.0 ** 60)
DFF = 512
NF = DFF // P

NPART = 3
BLOCK_ROWS = NPART * DH
MASK_ROW = NPART * BLOCK_ROWS
KEY_ROWS = MASK_ROW + 1
MAX_ROW = KEY_ROWS
ALL_ROWS = MAX_ROW + NPART

ONES = 0x3F803F80

NLAYER = 5
NSTEP = NLAYER * B
CAUSAL, GIVEN, KEYS, WINDOW = range(4)
KIND = [CAUSAL, GIVEN, KEYS, WINDOW, GIVEN]
CROSS = [False, False, True, False, True]
SEGMENTS = [(0, 3 * B), (3 * B, NSTEP)]
AFFINE = {1: 0, 2: 1}

E0, G0, K0, H0 = 32, 8, 4, 256
CAP = max(1, int(B * S / E0 * K0 * 1.25))
SLOTS = E0 * CAP
ST = SLOTS // P
HC = CAP // 2
BITS = 30
FAR = 1.0e6
GRP = 2
NGRP = E0 // GRP
WRING = 3
E1, K1 = 8, 256


def build(nc: bass.Bass, a, out):
    ctx = ExitStack()
    with ctx:
        def sb(name, shape, dt=F32):
            return ctx.enter_context(nc.sbuf_tensor(name, shape, dt))

        def pb(name, shape, dt=F32):
            return ctx.enter_context(nc.psum_tensor(name, shape, dt))

        def sem(name):
            return ctx.enter_context(nc.semaphore(name))

        def dram(name, shape, dt=F32):
            return nc.dram_tensor(name, shape, dt, kind="Internal").ap()

        q_parts_dram = dram("q_parts_dram", (2, NPART, P, S), BF16)
        k_parts_dram = dram("k_parts_dram", (2, 3, P, S), BF16)
        key_mask_dram = dram("key_mask_dram", (B + 1, S), BF16)
        slot_x_dram = dram("slot_x_dram", (SLOTS, D))
        slot_y_dram = dram("slot_y_dram", (SLOTS, D))

        X = sb("X", [P, NT, D])
        XI = sb("XI", [P, NT, D])
        ctx_rows = sb("ctx_rows", [P, NT, D])
        ctxT = sb("ctxT", [P, B, S])
        xT = sb("xT", [P, 2, S])
        ident = sb("ident", [P, P])
        ident_b = sb("ident_b", [P, P], BF16)
        tri = sb("tri", [P, 2, P], BF16)
        given = sb("given", [P, QB, S], BF16)
        givenT = sb("givenT", [P, QB, S], BF16)
        given_i = sb("given_i", [P, QB, S], I32)
        keys_i = sb("keys_i", [B, S], I32)
        keys_row = sb("keys_row", [B + 1, S], BF16)
        neg_half = sb("neg_half", [P, NT])
        Wq = sb("Wq", [P, NLAYER, D])
        Wk = sb("Wk", [P, NLAYER, D])
        Wv = sb("Wv", [P, NLAYER, D])
        Wo = sb("Wo", [P, NLAYER, D])
        w_rows = sb("w_rows", [P, 8, D])
        bqk = sb("bqk", [P, NLAYER, 2])
        bvo = sb("bvo", [P, NLAYER, 2, D])
        ln_gb = sb("ln_gb", [P, 3, 2, D])
        stackQ = sb("stackQ", [ALL_ROWS, 3, NH, S], BF16)
        stackK = sb("stackK", [ALL_ROWS, 3, NH, S], BF16)
        q_parts = sb("q_parts", [P, 2, 3, S], BF16)
        k_parts = sb("k_parts", [P, 2, 3, S], BF16)
        q_rest = sb("q_rest", [P, 2, S])
        k_rest = sb("k_rest", [P, 2, S])
        v_aug = sb("v_aug", [P, 3, QB, NH, 32])
        mx = sb("mx", [P, QB, NH])
        m_rest = sb("m_rest", [P, QB, NH])
        m_parts = sb("m_parts", [P, 2, QB, 3, NH], BF16)
        mT = sb("mT", [3 * NH, 2, S], BF16)
        arena = sb("arena", [P, 6 * 4 * S])
        probsT = arena[:, 0:3 * 4 * S].rearrange("p (n j q) -> p n j q", n=3, j=4)
        oT = arena[:, 3 * 4 * S:4 * 4 * S].rearrange("p (n g q) -> p n g q", n=2, g=2)
        inv_den = sb("inv_den", [P, 2, QB, 8])
        o_rows = sb("o_rows", [P, 2, QB, D])
        nT = sb("nT", [P, 2, S])
        res = sb("res", [P, 2, QB, D])
        stats = sb("stats", [P, 2, QB, 6])
        mv = sb("mv", [P, 2, QB, 2])
        var_eps = sb("var_eps", [P, 2, QB])
        rstd = sb("rstd", [P, 2, QB])

        ff_w1 = sb("ff_w1", [P, DFF])
        ff_w2 = sb("ff_w2", [P, NF, D])
        ff_b1 = sb("ff_b1", [P, NF])
        ff_b2 = sb("ff_b2", [P, D])
        ff_h = arena[:, 4 * 4 * S:6 * 4 * S].rearrange("p (n f q) -> p n f q", n=2, f=NF)
        xT_all = sb("xT_all", [P, B * S])
        cent = sb("cent", [G0 + E0, D])
        cent_sq = sb("cent_sq", [G0 + E0, D])
        cent_n = sb("cent_n", [G0 + E0, 2])
        centT = sb("centT", [P, G0 + E0])
        bias0 = sb("bias0", [P, E0])
        sq = w_rows[:, :, :]
        norm_x = sb("norm_x", [P, 2, NT])
        scs = sb("scs", [P, NT, G0 + E0])
        g_gt = sb("g_gt", [P, NT, G0, G0])
        g_eq = sb("g_eq", [P, NT, G0, G0])
        lower = sb("lower", [P, G0, G0])
        g_rank = sb("g_rank", [P, NT, G0])
        g_in = sb("g_in", [P, NT, G0])
        g_pen = sb("g_pen", [P, NT, G0])
        top_v = sb("top_v", [P, NT, 8])
        top_i = sb("top_i", [P, NT, 8], U32)
        top_f = sb("top_f", [P, NT, K0])
        gate = sb("gate", [P, NT, K0])
        gate_sum = sb("gate_sum", [P, 2, NT])
        iota_e = sb("iota_e", [P, E0])
        hot = sb("hot", [P, NT * K0, E0])
        hot_pos = w_rows[:, :, :].rearrange("p a (b e) -> p (a b) e", e=E0)
        chosen = sb("chosen", [P, NT, E0], BF16)
        before_b = sb("before_b", [P, P], BF16)
        ones_b = sb("ones_b", [P, P], BF16)
        pos = sb("pos", [P, NT * K0])
        over = sb("over", [P, NT * K0])
        slot = sb("slot", [P, 3, NT * K0])
        slot_to = sb("slot_to", [P, NT * K0], U32)
        slot_from = sb("slot_from", [P, NT * K0], U32)
        sh_g = sb("sh_g", [P, H0])
        sh_u = sb("sh_u", [P, H0])
        sh_d = sb("sh_d", [P, 2, D])
        slot_rows = sb("slot_rows", [P, 2, 8, D])
        slotT = arena[:, 0:SLOTS]
        y_chosen = arena[:, 0:NT * K0 * D].rearrange("p (j d) -> p j d", d=D)
        silu_e = arena[:, SLOTS:SLOTS + 4 * CAP].rearrange("p (n c) -> p n c", n=2)
        silu_sh = arena[:, 2 * B * S:4 * B * S].rearrange("p (c h n) -> p c h n", c=2, h=2)
        wg_b = sb("wg_b", [P, WRING, GRP, H0])
        wu_b = sb("wu_b", [P, WRING, GRP, H0])
        wd_b = sb("wd_b", [P, WRING, GRP, 2, D])
        hT = sb("hT", [P, 2, 2, CAP])
        y_rows = sb("y_rows", [HC, 2, 2, D])
        Y = ctx_rows
        w1_b = wg_b[:, :, :, :].rearrange("p r e n -> p r (e n)")
        w2_b = wd_b[:, :, :, :, :].rearrange("p r e h d -> p r (e h) d")
        h1 = arena[:, 0:8 * 512].rearrange("p (n f t) -> p n f t", n=2, f=NF)
        router = sb("router", [P, E1])
        router_bias = sb("router_bias", [P, E1])
        b1_rows = sb("b1_rows", [E1 * NF, P])
        b1_cols = sb("b1_cols", [P, E1 * NF])
        b2_rows = sb("b2_rows", [E1, D])
        G = sb("G", [P, NT, E1])
        g_top = sb("g_top", [P, NT])
        flag = sb("flag", [P, 2, NT, E1])
        flag_sum = sb("flag_sum", [P, E1], BF16)
        equal = sb("equal", [P, NT, E1], BF16)
        low_cut = sb("low_cut", [P, E1])
        try_cut = sb("try_cut", [P, E1])
        try_ok = sb("try_ok", [P, E1])
        wT = slot_rows[0:E1, 0, :, :].rearrange("p t d -> p (t d)")
        ps = pb("ps", [P, 8, 512])
        psM = ps[:, 0:3, :]
        psE = ps[:, 3:6, :]
        psO = ps[:, 6, :].rearrange("p (g q) -> p g q", g=2)
        psX = ps[:, 7, :].rearrange("p (a q) -> p a q", a=2)
        psW = ps[:, 2:6, :].rearrange("p (a b) n -> p a (b n)", a=2)
        psA, psB = psX[:, 0, :], psX[:, 1, :]

        pos_ps = ps[:, 7, :][:, 0:NT * E0].rearrange("p (t e) -> p t e", t=NT)
        rs_ps = ps[:, 7, :][:, 0:NT * (G0 + E0)].rearrange("p (t e) -> p t e", t=NT)
        psE4 = ps[:, 2:6, :]
        sh_hT = slotT[:, 0:2 * B * S].rearrange("p (h t) -> p h t", h=2)

        names = {}

        def s_(name):
            if name not in names:
                names[name] = sem(name)
            return names[name]

        const_ready = s_("const_ready")
        x_loaded, ctx_loaded, wr_loaded, mask_loaded, q_rows_ready, k_rows_ready, v_const, mix_const = map(s_, (
            "x_loaded", "ctx_loaded", "wr_loaded", "mask_loaded", "q_rows_ready", "k_rows_ready", "v_const", "mix_const"))
        w_loaded = [s_(f"w_loaded{layer}") for layer in range(NLAYER)]
        keys_made, keys_stored, given_made, setup_pe, setup_act = map(s_, (
            "keys_made", "keys_stored", "given_made", "setup_pe", "setup_act"))
        x_ready, q_mid, k_mid = map(s_, ("x_ready", "q_mid", "k_mid"))
        t_done, xT_ready, q_done, k_done, v_done, q_hi, k_hi = map(s_, (
            "t_done", "xT_ready", "q_done", "k_done", "v_done", "q_hi", "k_hi"))
        q_resid, k_resid, v_ready, q_split, k_split = map(s_, (
            "q_resid", "k_resid", "v_ready", "q_split", "k_split"))
        q_stored, k_stored = map(s_, ("q_stored", "k_stored"))
        stack_loaded = [s_(f"stack_loaded{j}") for j in range(3)]
        m_loaded = [s_(f"m_loaded{j}") for j in range(2)]
        m_full, m_used, mx_done, m_split, mt_done, mT_ready = map(s_, (
            "m_full", "m_used", "mx_done", "m_split", "mt_done", "mT_ready"))
        e_full, exp_done, pv_done, oT_ready = map(s_, ("e_full", "exp_done", "pv_done", "oT_ready"))
        nt_done, nT_ready, wo_done, wo_read = map(s_, (
            "nt_done", "nT_ready", "wo_done", "wo_read"))
        pool_chain, dve_chain, rstd_ready, var_ready = map(s_, ("pool_chain", "dve_chain", "rstd_ready", "var_ready"))
        out_stored = s_("out_stored")

        f_xT, f_turned, f_up, f_h, f_down, f_read, ff_loaded = map(s_, (
            "f_xT", "f_turned", "f_up", "f_h", "f_down", "f_read", "ff_loaded"))
        x3_ready, moe0_ready, r_loaded, zero_ready, zero_stored = map(s_, (
            "x3_ready", "moe0_ready", "r_loaded", "zero_ready", "zero_stored"))
        xa_turned, xa_ready, cent_turned, centT_ready, cent_ready, rscore_done, rscore_read = map(s_, (
            "xa_turned", "xa_ready", "cent_turned", "centT_ready", "cent_ready", "rscore_done", "rscore_read"))
        pow_in, pow_out, gate_in, gate_exp, chosen_ready, pos_done, slots_ready, scattered = map(s_, (
            "pow_in", "pow_out", "gate_in", "gate_exp", "chosen_ready", "pos_done", "slots_ready", "scattered"))
        sh_up, sh_silu, sh_h, sh_down, sh_read = map(s_, ("sh_up", "sh_silu", "sh_h", "sh_down", "sh_read"))
        slots_loaded = [s_(f"slots_loaded{j}") for j in range(ST // 8)]
        slots_turned, slotT_ready = s_("slots_turned"), s_("slotT_ready")
        we_loaded = [s_(f"we_loaded{j}") for j in range(WRING)]
        e_up, e_silu, e_h, e_down, e_rows = map(s_, ("e_up", "e_silu", "e_h", "e_down", "e_rows"))
        y_stored = [s_(f"y_stored{j}") for j in range(2)]
        gathered = [s_(f"gathered{j}") for j in range(NT)]

        m1_loaded, l_done, l_exp_in, l_exp, b1_turned, b1_ready, try_ready, try_counted = map(s_, (
            "m1_loaded", "l_done", "l_exp_in", "l_exp", "b1_turned", "b1_ready", "try_ready", "try_counted"))
        eq_ready, eq_ranked, w_ready, w_turned, wT_ready, b2_done, b2_read = map(s_, (
            "eq_ready", "eq_ranked", "w_ready", "w_turned", "wT_ready", "b2_done", "b2_read"))
        w1_loaded = [s_(f"w1_loaded{j}") for j in range(WRING)]
        d_up, d_relu, d_down, d_read, final_ready = map(s_, ("d_up", "d_relu", "d_down", "d_read", "final_ready"))
        def x_in(layer):
            return XI if layer == 2 else X

        def x_out(layer):
            return XI if layer in (1, 2) else X

        def qlen(layer, kb):
            return kb if KIND[layer] in (CAUSAL, WINDOW) else 0

        def klen(layer, qb):
            return (qb + 1) * P if KIND[layer] in (CAUSAL, WINDOW) else S

        def m_order(lo, hi):
            for i in range(lo - 2, hi + 1):
                if lo <= i - 1 < hi:
                    yield ("o", i - 1, 1)
                if lo <= i + 1 < hi:
                    for c in range(16):
                        yield ("s", i + 1, c)
                if lo <= i < hi:
                    yield ("o", i, 0)

        m_at = {key: n for n, key in enumerate(k for lo, hi in SEGMENTS for k in m_order(lo, hi))}
        SCORES_IN_SLOT = [2, 1, 2, 1, 2, 1, 2, 1, 2, 1, 1, 0, 0, 0, 0, 0]
        TURN_X, PROJ_Q, PROJ_K, PROJ_V, TURN_NORMED, PROJ_OUT, TURN_OUT, TURN_MAX = 0, 2, 4, 6, 8, 10, 11, 14

        def sends_mask(n):
            return n < 3 or KIND[n // B] == KEYS or KIND[(n - 3) // B] == KEYS

        def loads_until(n):
            return sum(2 * NPART + sends_mask(j) for j in range(n % 3, n + 1, 3))

        block = ctx.enter_context(nc.Block())

        W_NAMES = [("L0_attn_Wq", "L0_attn_Wk", "L0_attn_Wv", "L0_attn_Wo"),
                   ("L0_xattn_s_wq", "L0_xattn_s_wk", "L0_xattn_s_wv", "L0_xattn_s_wo"),
                   ("L0_xattn_c_wq", "L0_xattn_c_wk", "L0_xattn_c_wv", "L0_xattn_c_wo")]
        BIAS = {(0, 3): "L0_attn_bo",
                (1, 0): "L0_xattn_s_bq", (1, 1): "L0_xattn_s_bk", (1, 2): "L0_xattn_s_bv", (1, 3): "L0_xattn_s_bo",
                (2, 0): "L0_xattn_c_bq", (2, 1): "L0_xattn_c_bk", (2, 2): "L0_xattn_c_bv", (2, 3): "L0_xattn_c_bo",
                (4, 0): "L1_xattn_bq", (4, 1): "L1_xattn_bk", (4, 2): "L1_xattn_bv", (4, 3): "L1_xattn_bo"}
        W_LOADS = [5, 10, 10, 4, 4]
        row = lambda v: v.rearrange("(a n) -> a n", a=1)
        col = lambda v: v.rearrange("(n a) -> n a", a=1)

        @block.sync
        def _(sp):
            def load_weights(layer):
                if layer < 3:
                    for w, name in zip((Wq, Wk, Wv, Wo), W_NAMES[layer]):
                        sp.dma_start(w[:, layer, :], a[name]).then_inc(w_loaded[layer], 16)
                for c in range(4):
                    if layer == 3:
                        bias = a["L1_attn_b_out"] if c == 3 else a["L1_attn_b_in"][c * P:(c + 1) * P]
                    elif (layer, c) in BIAS:
                        bias = a[BIAS[layer, c]]
                    else:
                        continue
                    if c < 2:
                        sp.dma_start(bqk[:, layer, c:c + 1], col(bias))\
                            .then_inc(w_loaded[layer], 16)
                    else:
                        sp.dma_start(bvo[:, layer, c - 2, :], row(bias).broadcast_to([P, D])).then_inc(w_loaded[layer], 16)
                if layer in AFFINE:
                    load_gain(AFFINE[layer], w_loaded[layer])

            def load_gain(n, sem):
                for c, g in enumerate("gb"):
                    sp.dma_start(ln_gb[:, n, c, :], row(a[f"L0_xattn_ln{n + 1}_{g}"]).broadcast_to([P, D]))\
                        .then_inc(sem, 16)

            def load_others():
                sp.dma_start(ff_w1[:, :], a["L0_xattn_ff_w1"]).then_inc(ff_loaded, 16)
                sp.dma_start(ff_w2[:, :, :], a["L0_xattn_ff_w2"].rearrange("(f p) d -> p f d", p=P)).then_inc(ff_loaded, 16)
                for f in range(NF):
                    sp.dma_start(ff_b1[:, f:f + 1], col(a["L0_xattn_ff_b1"][f * P:(f + 1) * P])).then_inc(ff_loaded, 16)
                sp.dma_start(ff_b2[:, :], row(a["L0_xattn_ff_b2"]).broadcast_to([P, D])).then_inc(ff_loaded, 16)
                load_gain(2, ff_loaded)
                sp.dma_start(cent[0:G0, :], a["L0_ffn_group_centroids"]).then_inc(r_loaded, 16)
                sp.dma_start(cent[G0:G0 + E0, :], a["L0_ffn_expert_centroids"]).then_inc(r_loaded, 16)
                sp.dma_start(bias0[:, :], row(a["L0_ffn_bias"]).broadcast_to([P, E0])).then_inc(r_loaded, 16)
                sp.dma_start(sh_g[:, :], a["L0_ffn_sg"]).then_inc(r_loaded, 16)
                sp.dma_start(sh_u[:, :], a["L0_ffn_su"]).then_inc(r_loaded, 16)
                sp.dma_start(sh_d[:, :, :], a["L0_ffn_sd"].rearrange("(h p) d -> p h d", p=P)).then_inc(r_loaded, 16)
                sp.dma_start(router[:, :], a["L1_ffn_router_w"]).then_inc(m1_loaded, 16)
                sp.dma_start(router_bias[:, :], row(a["L1_ffn_router_b"]).broadcast_to([P, E1])).then_inc(m1_loaded, 16)
                sp.dma_start(b1_rows[:, :], a["L1_ffn_b1"].rearrange("e (f p) -> (e f) p", p=P)).then_inc(m1_loaded, 16)
                sp.dma_start(b2_rows[:, :], a["L1_ffn_b2"]).then_inc(m1_loaded, 16)
                clear_slots()

            sp.dma_start(X[:, :, :], a["x"].rearrange("b (t p) d -> p (b t) d", p=P)).then_inc(x_loaded, 16)
            load_weights(0)
            sp.dma_start(w_rows[:, 0:3, :], a["L1_attn_w_in"].rearrange("(c p) d -> p c d", p=P)).then_inc(wr_loaded, 16)
            sp.dma_start(w_rows[:, 3, :], a["L1_attn_w_out"]).then_inc(wr_loaded, 16)
            for c, name in enumerate(("L1_xattn_Wq", "L1_xattn_Wk", "L1_xattn_Wv", "L1_xattn_Wo")):
                sp.dma_start(w_rows[:, 4 + c, :], a[name]).then_inc(wr_loaded, 16)
            sp.dma_start(ctx_rows[:, :, :], a["ctx_1024"].rearrange("b (t p) d -> p (b t) d", p=P))\
                .then_inc(ctx_loaded, 16)
            sp.wait_ge(keys_made, 1)
            sp.dma_start(key_mask_dram, keys_row[:, :]).then_inc(keys_stored, 16)

            def clear_slots():
                sp.wait_ge(zero_ready, 1)
                for j in range(ST // 8):
                    sp.dma_start(slot_x_dram[8 * j * P:8 * (j + 1) * P, :].rearrange("(p t) d -> p t d", p=P),
                                 slot_rows[:, 0, :, :]).then_inc(zero_stored, 16)

            def load_experts(g):
                if g >= WRING:
                    sp.wait_ge(e_down, GRP * (g - WRING + 1))
                r, e = g % WRING, slice(GRP * g, GRP * (g + 1))
                sp.dma_start(wg_b[:, r, :, :], a["L0_ffn_wg"][e].rearrange("e d h -> d e h")).then_inc(we_loaded[r], 16)
                sp.dma_start(wu_b[:, r, :, :], a["L0_ffn_wu"][e].rearrange("e d h -> d e h")).then_inc(we_loaded[r], 16)
                sp.dma_start(wd_b[:, r, :, :, :], a["L0_ffn_wd"][e].rearrange("e (h p) d -> p e h d", p=P))\
                    .then_inc(we_loaded[r], 16)

            def first_mixture():
                for g in range(WRING):
                    load_experts(g)
                sp.wait_ge(scattered, 16 * NT * K0)
                for j in range(ST // 8):
                    if j >= 2:
                        sp.wait_ge(slots_turned, j - 1)
                    sp.dma_start(slot_rows[:, j % 2, :, :],
                                 slot_x_dram[8 * j * P:8 * (j + 1) * P, :].rearrange("(t p) d -> p t d", p=P))\
                        .then_inc(slots_loaded[j], 16)
                for e in range(E0):
                    sp.wait_ge(e_rows, e + 1)
                    sp.dma_start(slot_y_dram[e * CAP:(e + 1) * CAP, :].rearrange("(c p) d -> p c d", p=HC),
                                 y_rows[:, e % 2, :, :]).then_inc(y_stored[e % 2], 16)
                    if e % GRP == GRP - 1 and e // GRP + WRING < NGRP:
                        load_experts(e // GRP + WRING)

            def send_parts(n):
                buf, par, r = n % 3, n % 2, n % B if KIND[n // B] == KEYS else B
                for split, parts, scratch, stored in ((q_split, q_parts, q_parts_dram, q_stored),
                                                      (k_split, k_parts, k_parts_dram, k_stored)):
                    sp.wait_ge(split, n + 1)
                    sp.dma_start(scratch[par].rearrange("s p t -> p s t"), parts[:, par, :, :]).then_inc(stored, 16)
                if n >= 3:
                    sp.wait_ge(e_full, 16 * (n - 2))
                else:
                    sp.wait_ge(q_rows_ready, n + 1)
                    sp.wait_ge(k_rows_ready, n + 1)
                if sends_mask(n):
                    if n == 0:
                        sp.wait_ge(keys_stored, 16)
                    sp.dma_start(stackK[MASK_ROW:MASK_ROW + 1, buf, :, :],
                                 key_mask_dram[r:r + 1, :].rearrange("a (o t) -> a o t", o=1).broadcast_to([1, NH, S]))\
                        .then_inc(stack_loaded[buf], 16)
                sp.wait_ge(q_stored, 16 * (n + 1))
                for b in range(NPART):
                    sp.dma_start(stackQ[BLOCK_ROWS * b:BLOCK_ROWS * (b + 1), buf, :, :],
                                 q_parts_dram[par].rearrange("a (d h) t -> d a (h t)", d=DH))\
                        .then_inc(stack_loaded[buf], 16)
                sp.wait_ge(k_stored, 16 * (n + 1))
                for b in range(NPART):
                    sp.dma_start(stackK[BLOCK_ROWS * b:BLOCK_ROWS * (b + 1), buf, :, :],
                                 k_parts_dram[par, b].rearrange("(d o h) t -> d o (h t)", d=DH, o=1)
                                 .broadcast_to([DH, NPART, NH * S])).then_inc(stack_loaded[buf], 16)

            def send_max(n):
                sp.wait_ge(mT_ready, n + 1)
                sp.dma_start(stackQ[MAX_ROW:ALL_ROWS, n % 3, :, :], mT[:, n % 2, :]).then_inc(m_loaded[n % 2], 16)

            def load_expert1(e):
                if e < WRING:
                    sp.wait_ge(e_down, E0)
                else:
                    sp.wait_ge(d_down, 2 * (e - WRING + 1))
                r = e % WRING
                sp.dma_start(w1_b[:, r, :], a["L1_ffn_w1"][e]).then_inc(w1_loaded[r], 16)
                sp.dma_start(w2_b[:, r, :, :], a["L1_ffn_w2"][e].rearrange("(f p) d -> p f d", p=P)).then_inc(w1_loaded[r], 16)

            for lo, hi in SEGMENTS:
                for i in range(lo - 2, hi):
                    if i + 2 < hi:
                        send_parts(i + 2)
                    if lo == 0 and i + 2 < 4:
                        load_weights(i + 3)
                    if lo == 0 and i + 2 == 4:
                        load_others()
                    if lo <= i + 1 < hi:
                        send_max(i + 1)
                if lo == 0:
                    first_mixture()
            for e in range(E1):
                load_expert1(e)
            sp.wait_ge(final_ready, B)
            sp.dma_start(out.rearrange("b (t p) d -> p (b t) d", p=P), X[:, :, :]).then_inc(out_stored, 16)
            sp.wait_ge(out_stored, 16)

        @block.tensor
        def _(pe):
            def turn_inputs():
                pe.wait_ge(wr_loaded, 16 * 6)
                for c in range(8):
                    if c >= 2:
                        pe.wait_ge(setup_act, c - 1)
                    pe.transpose(psM[:, c % 2, 0:P], w_rows[:, c, :], ident[:, :]).then_inc(setup_pe, 1)
                pe.wait_ge(ctx_loaded, 16)
                for b in range(B):
                    pe.wait_ge(setup_act, 8 + b - 1)
                    for t in range(QB):
                        mm = pe.transpose(psM[:, b % 2, t * P:(t + 1) * P], ctx_rows[:, QB * b + t, :], ident[:, :])
                    mm.then_inc(setup_pe, 1)
                pe.wait_ge(given_made, 1)
                pe.wait_ge(setup_act, 12)
                for kb in range(QB):
                    for qb in range(QB):
                        mm = pe.transpose(psM[:, kb, 0:P].bitcast(BF16)[:, qb * P:(qb + 1) * P],
                                          given[:, qb, kb * P:(kb + 1) * P], ident_b[:, :])
                mm.then_inc(setup_pe, 1)
                pe.wait_ge(setup_act, 13)

            def turn_x(n):
                if n < B:
                    pe.wait_ge(x_loaded, 16)
                elif n >= SEGMENTS[1][0] and n < SEGMENTS[1][0] + B:
                    pe.wait_ge(moe0_ready, n - SEGMENTS[1][0] + 1)
                else:
                    pe.wait_ge(x_ready, n - B + 1)
                if n - 2 >= lo_of(n):
                    pe.wait_ge(mT_ready, n - 1)
                elif n >= 1:
                    pe.wait_ge(v_ready, n)
                for t in range(QB):
                    mm = pe.transpose(psA[:, t * P:(t + 1) * P], x_in(n // B)[:, QB * (n % B) + t, :], ident[:, :])
                mm.then_inc(t_done, 1)

            def project_q(n):
                if n % B == 0:
                    pe.wait_ge(w_loaded[n // B], 16 * W_LOADS[n // B])
                pe.wait_ge(xT_ready, n + 1)
                pe.matmul(psB, Wq[:, n // B, :], xT[:, n % 2, :], start=True, stop=True).then_inc(q_done, 1)

            def source(n):
                return ctxT[:, n % B, :] if CROSS[n // B] else xT[:, n % 2, :]

            def project_k(n):
                pe.wait_ge(q_resid, n + 1)
                pe.matmul(psA, Wk[:, n // B, :], source(n), start=True, stop=True).then_inc(k_done, 1)

            def project_v(n):
                pe.wait_ge(k_resid, n + 1)
                for t in range(QB):
                    mm = pe.matmul(psB[:, t * P:(t + 1) * P], source(n)[:, t * P:(t + 1) * P], Wv[:, n // B, :],
                                   start=True, stop=True)
                mm.then_inc(v_done, 1)

            def score_chunk(n, c):
                layer, buf, qb, kw = n // B, n % 3, c // 8, klen(n // B, c // 8)
                at = m_at["s", n, c]
                if c == 0:
                    pe.wait_ge(stack_loaded[buf], 16 * loads_until(n))
                if at >= 3:
                    pe.wait_ge(m_used, at - 2)
                kind = KIND[layer]
                for j in range(2):
                    h = 2 * (c % 8) + j
                    dst = psM[:, at % 3, j * S:j * S + kw]
                    mm = pe.matmul(dst, stackQ[0:KEY_ROWS, buf, h, qb * P:(qb + 1) * P],
                                   stackK[0:KEY_ROWS, buf, h, 0:kw], start=True, stop=kind == KEYS)
                    if kind == GIVEN:
                        mm = pe.matmul(dst, ident_b[:, :], given[:, qb, :], start=False, stop=True)
                    if kind in (CAUSAL, WINDOW):
                        far = kind == WINDOW and qb == 1
                        mm = pe.matmul(dst[:, qb * P:(qb + 1) * P], ident_b[:, :], tri[:, 0, :],
                                       start=False, stop=not far)
                        if far:
                            mm = pe.matmul(dst[:, 0:P], ident_b[:, :], tri[:, 1, :], start=False, stop=True)
                mm.then_inc(m_full, 1)

            def exp_chunk(n, j):
                layer, buf, unit = n // B, n % 3, j // 2
                g, kb, at, kind = unit // 2, unit % 2, 16 * n + j, KIND[n // B]
                q0 = qlen(layer, kb) * P
                if j == 0:
                    pe.wait_ge(m_loaded[n % 2], 16 * (n // 2 + 1))
                if at >= 3:
                    pe.wait_ge(exp_done, at - 2)
                for i in range(2):
                    h = 4 * g + 2 * (j % 2) + i
                    dst = psE[:, at % 3, i * S + q0:(i + 1) * S]
                    mm = pe.matmul(dst, stackK[:, buf, h, kb * P:(kb + 1) * P], stackQ[:, buf, h, q0:S],
                                   start=True, stop=kind == KEYS)
                    if kind == GIVEN:
                        mm = pe.matmul(dst, ident_b[:, :], givenT[:, kb, :], start=False, stop=True)
                    if kind in (CAUSAL, WINDOW):
                        far = kind == WINDOW and kb == 0
                        mm = pe.matmul(dst[:, 0:P], ident_b[:, :], tri[:, 1, :], start=False, stop=not far)
                        if far:
                            mm = pe.matmul(dst[:, P:2 * P], ident_b[:, :], tri[:, 0, :], start=False, stop=True)
                mm.then_inc(e_full, 1)

            def values_unit(n, c):
                g, kb, at = c // 2, c % 2, 8 * n + c
                q0 = qlen(n // B, kb) * P
                if c == 0:
                    pe.wait_ge(v_ready, n + 1)
                if c % 4 == 0 and 2 * n + c // 4 > 0:
                    pe.wait_ge(oT_ready, 2 * n + c // 4)
                pe.wait_ge(exp_done, 2 * at + 2)
                for j in range(4):
                    mm = pe.matmul(psO[32 * j:32 * j + 32, g % 2, q0:S], v_aug[:, n % 3, kb, 4 * g + j, :],
                                   probsT[:, at % 3, j, q0:S], start=kb == 0, stop=kb == 1, skip_group_check=True)
                mm.then_inc(pv_done, 1)

            def turn_outputs(n, half):
                at = m_at["o", n, half]
                pe.wait_ge(oT_ready, 2 * n + half + 1)
                if at >= 3:
                    pe.wait_ge(m_used, at - 2)
                for gg in range(2):
                    for qb in range(QB):
                        i = 2 * gg + qb
                        mm = pe.transpose(psM[:, at % 3, i * P:(i + 1) * P], oT[:, half, gg, qb * P:(qb + 1) * P],
                                          ident[:, :])
                mm.then_inc(m_full, 1)

            def turn_normed(n):
                pe.wait_ge(m_used, m_at["o", n, 1] + 1)
                if n + 3 < hi_of(n):
                    pe.wait_ge(v_ready, n + 4)
                else:
                    pe.wait_ge(mT_ready, min(n + 2, hi_of(n)))
                    if n >= 1:
                        pe.wait_ge(wo_read, n)
                for t in range(QB):
                    mm = pe.transpose(psA[:, t * P:(t + 1) * P], o_rows[:, n % 2, t, :], ident[:, :])
                mm.then_inc(nt_done, 1)

            def project_out(n):
                pe.wait_ge(nT_ready, n + 1)
                for t in range(QB):
                    mm = pe.matmul(psB[:, t * P:(t + 1) * P], nT[:, n % 2, t * P:(t + 1) * P], Wo[:, n // B, :],
                                   start=True, stop=True)
                mm.then_inc(wo_done, 1)

            def turn_max(n):
                pe.wait_ge(m_split, n + 1)
                if n - 2 >= lo_of(n):
                    pe.wait_ge(wo_read, n - 1)
                elif n + 1 < hi_of(n):
                    pe.wait_ge(v_ready, n + 2)
                for qb in range(QB):
                    mm = pe.transpose(psA.bitcast(BF16)[0:3 * NH, qb * P:(qb + 1) * P],
                                      m_parts[:, n % 2, qb, :, :].rearrange("p a h -> p (a h)"), ident_b[:, :])
                mm.then_inc(mt_done, 1)

            def lo_of(n):
                return SEGMENTS[0][0] if n < SEGMENTS[0][1] else SEGMENTS[1][0]

            def hi_of(n):
                return SEGMENTS[0][1] if n < SEGMENTS[0][1] else SEGMENTS[1][1]

            def feed_forward():
                pe.wait_ge(x_ready, SEGMENTS[0][1])
                pe.wait_ge(ff_loaded, 16 * (5 + NF))
                for b in range(B + 1):
                    if b < B:
                        if b >= 1:
                            pe.wait_ge(f_xT, b)
                        for t in range(QB):
                            mm = pe.transpose(psA[:, t * P:(t + 1) * P],
                                              XI[:, QB * b + t, :], ident[:, :])
                        mm.then_inc(f_turned, 1)
                        pe.wait_ge(f_xT, b + 1)
                        if b >= 2:
                            pe.wait_ge(f_h, b - 1)
                        for f in range(NF):
                            mm = pe.matmul(psW[:, b % 2, f * S:(f + 1) * S], ff_w1[:, f * P:(f + 1) * P],
                                           xT[:, b % 2, :], start=True, stop=True)
                        mm.then_inc(f_up, 1)
                    if b >= 1:
                        pe.wait_ge(f_h, b)
                        if b >= 3:
                            pe.wait_ge(f_read, b - 2)
                        for t in range(QB):
                            for f in range(NF):
                                mm = pe.matmul(psM[:, (b - 1) % 2, t * P:(t + 1) * P],
                                               ff_h[:, (b - 1) % 2, f, t * P:(t + 1) * P], ff_w2[:, f, :],
                                               start=f == 0, stop=f == NF - 1)
                        mm.then_inc(f_down, 1)

            def turn_all(count):
                for t in range(NT):
                    mm = pe.transpose(psW[:, 0, t * P:(t + 1) * P], X[:, t, :], ident[:, :])
                mm.then_inc(xa_turned, 1)
                pe.wait_ge(xa_ready, count)

            def first_mixture():
                pe.wait_ge(cent_ready, 1)
                pe.transpose(psX[:, 0, 0:G0 + E0], cent_sq[:, :], ident[0:G0 + E0, 0:G0 + E0]).then_inc(cent_turned, 1)
                pe.wait_ge(x3_ready, B)
                turn_all(1)
                pe.wait_ge(centT_ready, 1)
                n = G0 + E0
                for t in range(NT):
                    mm = pe.matmul(ps[:, 7, :][:, t * n:(t + 1) * n],
                                   xT_all[:, t * P:(t + 1) * P], centT[:, :], start=True, stop=True)
                mm.then_inc(rscore_done, 1)
                for c in range(2):
                    if c == 1:
                        pe.wait_ge(sh_h, 1)
                    for w, half in ((sh_g, 0), (sh_u, 1)):
                        for h in range(2):
                            mm = pe.matmul(psW[:, half, h * 512:(h + 1) * 512], w[:, h * P:(h + 1) * P],
                                           xT_all[:, c * 512:(c + 1) * 512], start=True, stop=True)
                    mm.then_inc(sh_up, 1)
                pe.wait_ge(mix_const, 1)
                pe.wait_ge(chosen_ready, 1)
                for t in range(NT):
                    for t2 in range(t + 1):
                        mm = pe.matmul(pos_ps[:, t, :],
                                       before_b[:, :] if t2 == t else ones_b[:, :], chosen[:, t2, :],
                                       start=t2 == 0, stop=t2 == t)
                mm.then_inc(pos_done, 1)
                pe.wait_ge(sh_h, 2)
                for c in range(2):
                    for t in range(4):
                        for h in range(2):
                            mm = pe.matmul(psM[:, c, t * P:(t + 1) * P], sh_hT[:, h, (4 * c + t) * P:(4 * c + t + 1) * P],
                                           sh_d[:, h, :], start=h == 0, stop=h == 1)
                    mm.then_inc(sh_down, 1)
                for j in range(ST // 8):
                    pe.wait_ge(slots_loaded[j], 16)
                    if j >= 2:
                        pe.wait_ge(slotT_ready, j - 1)
                    for t in range(8):
                        mm = pe.transpose(psW[:, j % 2, t * P:(t + 1) * P], slot_rows[:, j % 2, t, :], ident[:, :])
                    mm.then_inc(slots_turned, 1)
                pe.wait_ge(slotT_ready, ST // 8)
                pe.wait_ge(sh_read, 2)
                for e in range(E0 + 1):
                    if e < E0:
                        r, j = e // GRP % WRING, e % GRP
                        if j == 0:
                            pe.wait_ge(we_loaded[r], 48 * (e // GRP // WRING + 1))
                        if e >= 2:
                            pe.wait_ge(e_h, e - 1)
                        for w, at in ((wg_b, 0), (wu_b, 512)):
                            for h in range(2):
                                mm = pe.matmul(psW[:, e % 2, at + h * CAP:at + (h + 1) * CAP],
                                               w[:, r, j, h * P:(h + 1) * P], slotT[:, e * CAP:(e + 1) * CAP],
                                               start=True, stop=True)
                        mm.then_inc(e_up, 1)
                    if e >= 1:
                        d = e - 1
                        r, j = d // GRP % WRING, d % GRP
                        pe.wait_ge(e_h, d + 1)
                        if d >= 2:
                            pe.wait_ge(e_rows, d - 1)
                        for c in range(2):
                            for h in range(2):
                                mm = pe.matmul(psM[0:HC, d % 2, c * P:(c + 1) * P],
                                               hT[:, d % 2, h, c * HC:(c + 1) * HC], wd_b[:, r, j, h, :],
                                               start=h == 0, stop=h == 1)
                        mm.then_inc(e_down, 1)

            def second_mixture():
                pe.wait_ge(m1_loaded, 64)
                pe.wait_ge(x_ready, NSTEP)
                pe.transpose(psX[:, 0, 0:E1 * NF], b1_rows[:, :], ident[0:E1 * NF, 0:E1 * NF]).then_inc(b1_turned, 1)
                turn_all(2)
                pe.wait_ge(b1_ready, 1)
                for t in range(NT):
                    mm = pe.matmul(psX[:, 0, t * E1:(t + 1) * E1], xT_all[:, t * P:(t + 1) * P], router[:, :],
                                   start=True, stop=True)
                mm.then_inc(l_done, 1)
                for n in range(BITS + 1):
                    pe.wait_ge(try_ready, n + 1)
                    pe.matmul(psM[:, n % 2, 0:E1], ones_b[:, :], flag_sum[:, :], start=True, stop=True)\
                        .then_inc(try_counted, 1)
                pe.wait_ge(eq_ready, 1)
                for t in range(NT):
                    for t2 in range(t + 1):
                        mm = pe.matmul(psX[:, 0, t * E1:(t + 1) * E1], before_b[:, :] if t2 == t else ones_b[:, :],
                                       equal[:, t2, :], start=t2 == 0, stop=t2 == t)
                mm.then_inc(eq_ranked, 1)
                pe.wait_ge(w_ready, 1)
                for t in range(NT):
                    mm = pe.transpose(psW[0:E1, 0, t * P:(t + 1) * P], G[:, t, :], ident[:, :])
                mm.then_inc(w_turned, 1)
                pe.wait_ge(wT_ready, 1)
                for c in range(2):
                    for t in range(4):
                        mm = pe.matmul(psM[:, c, t * P:(t + 1) * P], wT[:, (4 * c + t) * P:(4 * c + t + 1) * P],
                                       b2_rows[:, :], start=True, stop=True)
                    mm.then_inc(b2_done, 1)
                for u in range(2 * E1 + 1):
                    if u < 2 * E1:
                        e, c = u // 2, u % 2
                        r = e % WRING
                        if c == 0:
                            pe.wait_ge(w1_loaded[r], 32 * (e // WRING + 1))
                        for f in range(NF):
                            if u >= 1:
                                pe.wait_ge(d_relu, NF * (u - 1) + f + 1)
                            pe.matmul(psE4[:, f, :], w1_b[:, r, f * P:(f + 1) * P], xT_all[:, c * 512:(c + 1) * 512],
                                      start=True, stop=True).then_inc(d_up, 1)
                    if u >= 1:
                        v = u - 1
                        e, c = v // 2, v % 2
                        r = e % WRING
                        pe.wait_ge(d_relu, NF * (v + 1))
                        if v < 2:
                            pe.wait_ge(b2_read, v + 1)
                        else:
                            pe.wait_ge(d_read, v - 1)
                        for t in range(4):
                            for f in range(NF):
                                mm = pe.matmul(psM[:, c, t * P:(t + 1) * P], h1[:, c, f, t * P:(t + 1) * P],
                                               w2_b[:, r, f, :], start=f == 0, stop=f == NF - 1)
                        mm.then_inc(d_down, 1)

            pe.wait_ge(const_ready, 1)
            for lo, hi in SEGMENTS:
                for i in range(lo - 2, hi + 1):
                    early, mid, late, tail = i + 2 < hi, lo <= i + 1 < hi, lo <= i < hi, lo <= i - 1
                    chunk = 0
                    for j in range(16):
                        if j == TURN_X and early:
                            turn_x(i + 2)
                        if j == TURN_X and tail:
                            turn_outputs(i - 1, 1)
                        if j == PROJ_Q and early:
                            project_q(i + 2)
                        if j == PROJ_K and early:
                            project_k(i + 2)
                        if j == PROJ_V and early:
                            project_v(i + 2)
                        if j == TURN_NORMED and tail:
                            turn_normed(i - 1)
                        if j == PROJ_OUT and tail:
                            project_out(i - 1)
                        if j == TURN_OUT and late:
                            turn_outputs(i, 0)
                        if j == TURN_MAX and mid:
                            turn_max(i + 1)
                        if late:
                            exp_chunk(i, j)
                        if mid and SCORES_IN_SLOT[j] > 0:
                            score_chunk(i + 1, chunk)
                            chunk += 1
                        if late and j % 2 == 1 and j >= 3:
                            values_unit(i, (j - 3) // 2)
                        if mid and SCORES_IN_SLOT[j] > 1:
                            score_chunk(i + 1, chunk)
                            chunk += 1
                    if late:
                        values_unit(i, 7)
                    if i == -2:
                        turn_inputs()
                if lo == 0:
                    feed_forward()
                    first_mixture()
                else:
                    second_mixture()

        @block.scalar
        def _(act):
            def copy_inputs():
                for c in range(8):
                    act.wait_ge(setup_pe, c + 1)
                    dst = (Wq, Wk, Wv, Wo)[c % 4][:, 3 + c // 4, :]
                    act.activation(dst, psM[:, c % 2, 0:P], ACT.Copy).then_inc(setup_act, 1)
                for b in range(B):
                    act.wait_ge(setup_pe, 9 + b)
                    act.activation(ctxT[:, b, :], psM[:, b % 2, 0:S], ACT.Copy).then_inc(setup_act, 1)
                act.wait_ge(setup_pe, 13)
                for kb in range(QB):
                    mm = act.activation(givenT[:, kb, :], psM[:, kb, 0:P].bitcast(BF16), ACT.Copy)
                mm.then_inc(setup_act, 1)

            def copy_xT(n):
                act.wait_ge(t_done, n + 1)
                if n >= 2:
                    act.wait_ge(v_done, n - 1)
                act.activation(xT[:, n % 2, :], psA, ACT.Copy).then_inc(xT_ready, 1)

            def high_part(n, done, parts, ps, bias, stored, ready):
                act.wait_ge(done, n + 1)
                if n >= 2:
                    act.wait_ge(stored, 16 * (n - 1))
                if n // B == 0:
                    mm = act.activation(parts[:, n % 2, 0, :], ps, ACT.Copy)
                else:
                    mm = act.activation(parts[:, n % 2, 0, :], ps, ACT.Identity, bias=bias)
                mm.then_inc(ready, 1)

            def middle_part(n, resid, parts, restof, ready):
                act.wait_ge(resid, n + 1)
                act.activation(parts[:, n % 2, 1, :], restof[:, n % 2, :], ACT.Copy).then_inc(ready, 1)

            def exp_chunk(n, j):
                at, unit, q0 = 16 * n + j, 8 * n + j // 2, qlen(n // B, j // 2 % 2) * P
                i = 2 * (j % 2)
                act.wait_ge(e_full, at + 1)
                if unit >= 3:
                    act.wait_ge(pv_done, unit - 2)
                act.activation(probsT[:, unit % 3, i:i + 2, q0:S],
                               psE[:, at % 3, :].rearrange("p (h q) -> p h q", h=2)[:, :, q0:S],
                               ACT.Exp, scale=SCALE).then_inc(exp_done, 1)

            def copy_outputs(n, half):
                act.wait_ge(pv_done, 8 * n + 4 * half + 4)
                if n >= 1:
                    act.wait_ge(m_full, m_at["o", n - 1, half] + 1)
                act.activation(oT[:, half, :, :], psO[:, :, :], ACT.Copy).then_inc(oT_ready, 1)

            def copy_normed(n):
                act.wait_ge(nt_done, n + 1)
                act.activation(nT[:, n % 2, :], psA, ACT.Copy).then_inc(nT_ready, 1)

            def copy_max(n):
                act.wait_ge(mt_done, n + 1)
                if n >= 2:
                    act.wait_ge(m_loaded[n % 2], 16 * (n // 2))
                act.activation(mT[:, n % 2, :], psA.bitcast(BF16)[0:3 * NH, 0:S], ACT.Copy).then_inc(mT_ready, 1)

            def feed_forward():
                act.wait_ge(ff_loaded, 16 * (5 + NF))
                for b in range(B):
                    act.wait_ge(f_turned, b + 1)
                    if b >= 2:
                        act.wait_ge(f_up, b - 1)
                    act.activation(xT[:, b % 2, :], psA, ACT.Copy).then_inc(f_xT, 1)
                    act.wait_ge(f_up, b + 1)
                    if b >= 2:
                        act.wait_ge(f_down, b - 1)
                    for f in range(NF):
                        mm = act.activation(ff_h[:, b % 2, f, :], psW[:, b % 2, f * S:(f + 1) * S], ACT.Relu,
                                            bias=ff_b1[:, f:f + 1])
                    mm.then_inc(f_h, 1)

            def first_mixture():
                act.wait_ge(cent_turned, 1)
                act.activation(centT[:, :], psX[:, 0, 0:G0 + E0], ACT.Copy).then_inc(centT_ready, 1)
                act.wait_ge(xa_turned, 1)
                act.activation(xT_all[:, :], psW[:, 0, :], ACT.Copy).then_inc(xa_ready, 1)
                act.wait_ge(gate_in, 1)
                act.activation(gate[:, :, :], gate[:, :, :], ACT.Exp).then_inc(gate_exp, 1)
                for c in range(2):
                    act.wait_ge(sh_up, c + 1)
                    act.activation(silu_sh[:, c, :, :].rearrange("p h n -> p (h n)"), psW[:, 0, :], ACT.Silu)\
                        .then_inc(sh_silu, 1)
                for j in range(ST // 8):
                    if j == 0:
                        act.wait_ge(sh_down, 2)
                    act.wait_ge(slots_turned, j + 1)
                    act.activation(slotT[:, 8 * j * P:8 * (j + 1) * P], psW[:, j % 2, :], ACT.Copy).then_inc(slotT_ready, 1)
                for e in range(E0 + 1):
                    if e < E0:
                        act.wait_ge(e_up, e + 1)
                        if e >= 2:
                            act.wait_ge(e_h, e - 1)
                        act.activation(silu_e[:, e % 2, :], psW[:, e % 2, 0:2 * CAP], ACT.Silu).then_inc(e_silu, 1)
                    if e >= 1:
                        d = e - 1
                        act.wait_ge(e_down, d + 1)
                        if d >= 2:
                            act.wait_ge(y_stored[d % 2], 16 * (d // 2))
                        act.activation(y_rows[:, d % 2, :, :], psM[0:HC, d % 2, 0:2 * D].rearrange("p (c d) -> p c d", c=2),
                                       ACT.Copy).then_inc(e_rows, 1)

            def second_mixture():
                act.wait_ge(b1_turned, 1)
                act.activation(b1_cols[:, :], psX[:, 0, 0:E1 * NF], ACT.Copy).then_inc(b1_ready, 1)
                act.wait_ge(xa_turned, 2)
                act.activation(xT_all[:, :], psW[:, 0, :], ACT.Copy).then_inc(xa_ready, 1)
                act.wait_ge(l_exp_in, 1)
                act.activation(G[:, :, :], G[:, :, :], ACT.Exp).then_inc(l_exp, 1)
                act.wait_ge(w_turned, 1)
                act.activation(wT[:, :], psW[0:E1, 0, :], ACT.Copy).then_inc(wT_ready, 1)
                for u in range(2 * E1):
                    if u >= 2:
                        act.wait_ge(d_down, u - 1)
                    for f in range(NF):
                        act.wait_ge(d_up, NF * u + f + 1)
                        j = u // 2 * NF + f
                        act.activation(h1[:, u % 2, f, :], psE4[:, f, :], ACT.Relu, bias=b1_cols[:, j:j + 1])\
                            .then_inc(d_relu, 1)

            for lo, hi in SEGMENTS:
                for i in range(lo - 2, hi + 1):
                    early, mid, late, tail = i + 2 < hi, lo <= i + 1 < hi, lo <= i < hi, lo <= i - 1
                    n = i + 2
                    for j in range(16):
                        if j == TURN_X and early:
                            copy_xT(n)
                        if j == PROJ_Q and early:
                            if n % B == 0:
                                act.wait_ge(w_loaded[n // B], 16 * W_LOADS[n // B])
                            high_part(n, q_done, q_parts, psB, bqk[:, n // B, 0:1], q_stored, q_hi)
                        if j == PROJ_Q + 1 and early:
                            middle_part(n, q_resid, q_parts, q_rest, q_mid)
                        if j == PROJ_K and early:
                            high_part(n, k_done, k_parts, psA, bqk[:, n // B, 1:2], k_stored, k_hi)
                        if j == PROJ_K + 1 and early:
                            middle_part(n, k_resid, k_parts, k_rest, k_mid)
                        if j == TURN_NORMED and tail:
                            copy_normed(i - 1)
                        if j == TURN_OUT and late:
                            copy_outputs(i, 0)
                        if j == TURN_MAX and mid:
                            copy_max(i + 1)
                        if late:
                            exp_chunk(i, j)
                    if late:
                        copy_outputs(i, 1)
                    if i == -2:
                        copy_inputs()
                if lo == 0:
                    feed_forward()
                    first_mixture()
                else:
                    second_mixture()

        @block.vector
        def _(dve):
            chain = [0]

            def link(ins):
                chain[0] += 1
                ins.then_inc(dve_chain, 1)
                dve.wait_ge(dve_chain, chain[0])

            def rest(n, hi_ready, parts, restof, src, bias, ready, split):
                dve.wait_ge(hi_ready, n + 1)
                if n >= 2:
                    dve.wait_ge(split, n - 1)
                if n // B == 0:
                    dve.tensor_tensor(restof[:, n % 2, :], src, parts[:, n % 2, 0, :], ALU.subtract).then_inc(ready, 1)
                else:
                    dve.scalar_tensor_tensor(restof[:, n % 2, :], src, bias, parts[:, n % 2, 0, :],
                                             ALU.add, ALU.subtract).then_inc(ready, 1)

            def take_v(n):
                dve.wait_ge(v_done, n + 1)
                if n < 3:
                    dve.wait_ge(v_const, n + 1)
                if n >= 3:
                    dve.wait_ge(pv_done, 8 * (n - 2))
                dst = v_aug[:, n % 3, :, :, 0:DH]
                src = psB.rearrange("p (t h d) -> p t h d", t=QB, d=DH)
                if n // B == 0:
                    dve.tensor_copy(dst, src).then_inc(v_ready, 1)
                else:
                    bias = bvo[:, n // B, 0, :].rearrange("p (o h d) -> p o h d", o=1, d=DH).broadcast_to([P, QB, NH, DH])
                    dve.tensor_tensor(dst, src, bias, ALU.add).then_inc(v_ready, 1)

            def row_max(n, c):
                at, qb, kw = m_at["s", n, c], c // 8, klen(n // B, c // 8)
                dve.wait_ge(m_full, at + 1)
                h = 2 * (c % 8)
                mm = dve.tensor_reduce(mx[:, qb, h:h + 2],
                                       psM[:, at % 3, :].rearrange("p (h k) -> p h k", h=2)[:, :, 0:kw],
                                       AX, ALU.max, negate=True)
                mm.then_inc(m_used, 1)

            def split_max(n):
                if n >= 2:
                    dve.wait_ge(mt_done, n - 1)
                part = [m_parts[:, n % 2, :, c, :] for c in range(NPART)]
                dve.wait_ge(m_used, m_at["s", n, 15] + 1)
                link(dve.tensor_copy(part[0], mx[:, :, :]))
                link(dve.tensor_tensor(m_rest[:, :, :], mx[:, :, :], part[0], ALU.subtract))
                link(dve.tensor_copy(part[1], m_rest[:, :, :]))
                dve.tensor_tensor(part[2], m_rest[:, :, :], part[1], ALU.subtract).then_inc(m_split, 1)

            def norm_outputs(n, half):
                at = m_at["o", n, half]
                ps = psM[:, at % 3, :].rearrange("p (g q h e) -> p q g h e", g=2, q=QB, h=4)
                dve.wait_ge(m_full, at + 1)
                if n >= 2:
                    dve.wait_ge(nt_done, n - 1)
                for qb in range(QB):
                    mm = dve.reciprocal(inv_den[:, half, qb, :].rearrange("p (g h) -> p g h", g=2),
                                        ps[:, qb, :, :, DH])
                link(mm)
                for qb in range(QB):
                    dst = o_rows[:, n % 2, qb, half * 64:half * 64 + 64].rearrange("p (g h d) -> p g h d", g=2, h=4)
                    inv = inv_den[:, half, qb, :].rearrange("p (g h o) -> p g h o", g=2, o=1)\
                        .broadcast_to([P, 2, 4, DH])
                    mm = dve.tensor_tensor(dst, ps[:, qb, :, :, 0:DH], inv, ALU.mult)
                mm.then_inc(m_used, 1)

            def layer_norm(src, dst, par, gain=None):
                for t in range(QB):
                    mm = dve.bn_stats(stats[:, par, t, :], src[:, t, :])
                link(mm)
                for t in range(QB):
                    mm = dve.bn_aggr(mv[:, par, t, :], stats[:, par, t, :])
                link(mm)
                dve.tensor_scalar(var_eps[:, par, :], mv[:, par, :, 1], EPS, None, ALU.add).then_inc(var_ready, 1)
                norms[0] += 1
                dve.wait_ge(rstd_ready, norms[0])
                for t in range(QB):
                    mm = dve.tensor_scalar(dst[:, t, :], src[:, t, :], mv[:, par, t, 0:1], rstd[:, par, t:t + 1],
                                           ALU.subtract, ALU.mult)
                if gain is not None:
                    gb = [ln_gb[:, gain, c, :].rearrange("p (o d) -> p o d", o=1).broadcast_to([P, QB, D])
                          for c in range(2)]
                    link(mm)
                    link(dve.tensor_tensor(dst, dst, gb[0], ALU.mult))
                    mm = dve.tensor_tensor(dst, dst, gb[1], ALU.add)
                return mm

            norms = [0]

            def finish(n):
                layer, par, b = n // B, n % 2, n % B
                dve.wait_ge(wo_done, n + 1)
                xb, dst = x_in(layer)[:, QB * b:QB * (b + 1), :], x_out(layer)[:, QB * b:QB * (b + 1), :]
                bias = bvo[:, layer, 1, :].rearrange("p (o d) -> p o d", o=1).broadcast_to([P, QB, D])
                dve.tensor_tensor(res[:, par, :, :], psB.rearrange("p (t d) -> p t d", t=QB), bias, ALU.add)\
                    .then_inc(wo_read, 1)
                dve.wait_ge(wo_read, n + 1)
                link(dve.tensor_tensor(res[:, par, :, :], res[:, par, :, :], xb, ALU.add))
                layer_norm(res[:, par], dst, par, AFFINE.get(layer)).then_inc(x_ready, 1)

            def spread(v, shape):
                return v.broadcast_to(shape)

            def feed_forward():
                for b in range(B):
                    par = b % 2
                    xb, xi = X[:, QB * b:QB * (b + 1), :], XI[:, QB * b:QB * (b + 1), :]
                    r = res[:, par, :, :]
                    dve.wait_ge(f_down, b + 1)
                    bias = ff_b2[:, :].rearrange("p (o d) -> p o d", o=1).broadcast_to([P, QB, D])
                    dve.tensor_tensor(r, psM[:, par, 0:QB * D].rearrange("p (t d) -> p t d", t=QB), bias, ALU.add)\
                        .then_inc(f_read, 1)
                    dve.wait_ge(f_read, b + 1)
                    link(dve.tensor_tensor(r, r, xi, ALU.add))
                    link(layer_norm(r, r, par, 2))
                    link(dve.tensor_tensor(r, r, xb, ALU.add))
                    layer_norm(r, xb, par).then_inc(x3_ready, 1)

            def first_mixture():
                n = G0 + E0
                dve.wait_ge(mix_const, 1)
                dve.wait_ge(r_loaded, 16 * 6)
                link(dve.tensor_tensor(cent_sq[:, :], cent[:, :], cent[:, :], ALU.mult))
                link(dve.tensor_reduce(cent_n[:, 0:1], cent_sq[:, :], AX, ALU.add))
                dve.tensor_scalar(cent_n[:, 0:1], cent_n[:, 0:1], 1e-24, None, ALU.max).then_inc(pow_in, 1)
                dve.wait_ge(pow_out, 1)
                dve.tensor_scalar(cent_sq[:, :], cent[:, :], cent_n[:, 1:2], None, ALU.mult).then_inc(cent_ready, 1)
                link(dve.tensor_tensor(sq[:, :, :], X[:, :, :], X[:, :, :], ALU.mult))
                link(dve.tensor_reduce(norm_x[:, 0, :], sq[:, :, :], AX, ALU.add))
                dve.tensor_scalar(norm_x[:, 0, :], norm_x[:, 0, :], 1e-24, None, ALU.max).then_inc(pow_in, 1)
                dve.wait_ge(pow_out, 2)
                dve.wait_ge(rscore_done, 1)
                link(dve.tensor_tensor(scs[:, :, :], rs_ps, norm_x[:, 1, :].rearrange("p (t o) -> p t o", o=1)
                                       .broadcast_to([P, NT, n]), ALU.mult))
                gs = scs[:, :, 0:G0]
                gj = gs.rearrange("p t (o j) -> p t o j", o=1).broadcast_to([P, NT, G0, G0])
                gi = gs.rearrange("p t (i o) -> p t i o", o=1).broadcast_to([P, NT, G0, G0])
                dve.tensor_tensor(g_gt[:, :, :, :], gj, gi, ALU.is_gt)
                link(dve.tensor_tensor(g_eq[:, :, :, :], gj, gi, ALU.is_equal))
                low = lower[:, :, :].rearrange("p (o i) j -> p o i j", o=1).broadcast_to([P, NT, G0, G0])
                link(dve.tensor_tensor(g_eq[:, :, :, :], g_eq[:, :, :, :], low, ALU.mult))
                link(dve.tensor_tensor(g_gt[:, :, :, :], g_gt[:, :, :, :], g_eq[:, :, :, :], ALU.add))
                link(dve.tensor_reduce(g_rank[:, :, :], g_gt[:, :, :, :], AX, ALU.add))
                link(dve.tensor_scalar(g_in[:, :, :], g_rank[:, :, :], float(max(1, G0 // 2)), None, ALU.is_lt))
                dve.tensor_scalar(g_pen[:, :, :], g_in[:, :, :], 1e9, -1e9, ALU.mult, ALU.add)
                es = scs[:, :, G0:n]
                link(dve.tensor_tensor(es, es, bias0[:, :].rearrange("p (o e) -> p o e", o=1)
                                       .broadcast_to([P, NT, E0]), ALU.add))
                es4 = es.rearrange("p t (g c) -> p t g c", g=G0)
                sp4 = [NT, G0, E0 // G0]
                link(dve.tensor_tensor(es4, es4, g_in[:, :, :].rearrange("p t (g o) -> p t g o", o=1)
                                       .broadcast_to([P] + sp4), ALU.mult))
                link(dve.tensor_tensor(es4, es4, g_pen[:, :, :].rearrange("p t (g o) -> p t g o", o=1)
                                       .broadcast_to([P] + sp4), ALU.add))
                for t in range(NT):
                    mm = dve.max(top_v[:, t, :], scs[:, t, G0:n])
                link(mm)
                for t in range(NT):
                    mm = dve.max_index(top_i[:, t, :], top_v[:, t, :], scs[:, t, G0:n])
                link(mm)
                tv = top_v[:, :, 0:K0]
                dve.tensor_tensor(gate[:, :, :], tv, top_v[:, :, 0:1].broadcast_to([P, NT, K0]), ALU.subtract)\
                    .then_inc(gate_in, 1)
                link(dve.tensor_copy(top_f[:, :, :], top_i[:, :, 0:K0]))
                tf = top_f[:, :, :].rearrange("p t k -> p (t k)")
                NK = NT * K0
                link(dve.tensor_tensor(hot[:, :, :], iota_e[:, :].rearrange("p (o e) -> p o e", o=1)
                                       .broadcast_to([P, NK, E0]),
                                       tf.rearrange("p (k o) -> p k o", o=1).broadcast_to([P, NK, E0]), ALU.is_equal))
                hv = hot[:, :, :].rearrange("p (t k) e -> p t k e", k=K0)
                ch = hot_pos[:, 0:3 * NT, :].rearrange("p (c t) e -> p c t e", c=3)
                dve.tensor_tensor(ch[:, 0], hv[:, :, 0, :], hv[:, :, 1, :], ALU.add)
                link(dve.tensor_tensor(ch[:, 1], hv[:, :, 2, :], hv[:, :, 3, :], ALU.add))
                dve.tensor_tensor(chosen[:, :, :], ch[:, 0], ch[:, 1], ALU.add).then_inc(chosen_ready, 1)
                dve.wait_ge(chosen_ready, 1)
                dve.wait_ge(gate_exp, 1)
                link(dve.tensor_reduce(gate_sum[:, 0, :], gate[:, :, :], AX, ALU.add))
                link(dve.reciprocal(gate_sum[:, 1, :], gate_sum[:, 0, :]))
                link(dve.tensor_tensor(gate[:, :, :], gate[:, :, :], gate_sum[:, 1, :].rearrange("p (t o) -> p t o", o=1)
                                       .broadcast_to([P, NT, K0]), ALU.mult))
                shared_h(0)
                dve.wait_ge(pos_done, 1)
                pv4 = pos_ps.rearrange("p t (o e) -> p t o e", o=1).broadcast_to([P, NT, K0, E0])
                link(dve.tensor_tensor(hot_pos[:, :, :].rearrange("p (t k) e -> p t k e", k=K0), hv, pv4, ALU.mult))
                link(dve.tensor_reduce(pos[:, :], hot_pos[:, :, :], AX, ALU.add))
                dve.tensor_scalar(over[:, :], pos[:, :], float(CAP), None, ALU.is_ge)
                dve.tensor_scalar(slot[:, 0, :], pos[:, :], float(CAP - 1), None, ALU.min)
                link(dve.tensor_scalar(slot[:, 1, :], tf, float(CAP), None, ALU.mult))
                dve.tensor_tensor(slot[:, 0, :], slot[:, 0, :], slot[:, 1, :], ALU.add)
                link(dve.tensor_tensor(slot[:, 1, :], slot[:, 1, :], pos[:, :], ALU.add))
                link(dve.scalar_tensor_tensor(slot[:, 2, :], over[:, :], FAR, slot[:, 1, :], ALU.mult, ALU.add))
                dve.tensor_copy(slot_to[:, :], slot[:, 2, :])
                dve.tensor_copy(slot_from[:, :], slot[:, 0, :]).then_inc(slots_ready, 1)
                link(dve.tensor_scalar(over[:, :], over[:, :], -1.0, 1.0, ALU.mult, ALU.add))
                gf = gate[:, :, :].rearrange("p t k -> p (t k)")
                link(dve.tensor_tensor(gf, gf, over[:, :], ALU.mult))
                shared_h(1)
                for c in range(2):
                    dve.wait_ge(sh_down, c + 1)
                    dve.tensor_copy(Y[:, 4 * c:4 * c + 4, :], psM[:, c, :].rearrange("p (t d) -> p t d", t=4))\
                        .then_inc(sh_read, 1)
                for e in range(E0):
                    dve.wait_ge(e_silu, e + 1)
                    if e >= 2:
                        dve.wait_ge(e_down, e - 1)
                    dve.tensor_tensor(hT[:, e % 2, :, :].rearrange("p h c -> p (h c)"), silu_e[:, e % 2, :],
                                      psW[:, e % 2, 512:512 + 2 * CAP], ALU.mult).then_inc(e_h, 1)
                dve.wait_ge(sh_read, 2)
                for k in range(K0):
                    for t in range(NT):
                        if k == 0:
                            dve.wait_ge(gathered[t], 16 * K0)
                        mm = dve.scalar_tensor_tensor(Y[:, t, :], y_chosen[:, t * K0 + k, :], gate[:, t, k:k + 1],
                                                      Y[:, t, :], ALU.mult, ALU.add)
                    link(mm)
                link(dve.tensor_tensor(Y[:, :, :], Y[:, :, :], X[:, :, :], ALU.add))
                for b in range(B):
                    layer_norm(Y[:, QB * b:QB * (b + 1), :], X[:, QB * b:QB * (b + 1), :], b % 2).then_inc(moe0_ready, 1)

            def second_mixture():
                dve.wait_ge(m1_loaded, 64)
                dve.wait_ge(l_done, 1)
                one = lambda v: v.rearrange("p (t o) -> p t o", o=1).broadcast_to([P, NT, E1])
                every = lambda v: v.rearrange("p (o e) -> p o e", o=1).broadcast_to([P, NT, E1])
                link(dve.tensor_tensor(G[:, :, :], psX[:, 0, 0:NT * E1].rearrange("p (t e) -> p t e", t=NT),
                                       every(router_bias[:, :]), ALU.add))
                link(dve.tensor_reduce(g_top[:, :], G[:, :, :], AX, ALU.max))
                dve.tensor_tensor(G[:, :, :], G[:, :, :], one(g_top[:, :]), ALU.subtract).then_inc(l_exp_in, 1)
                dve.memset(low_cut[:, :], 0.0)
                link(dve.memset(try_cut[:, :].bitcast(I32), 1 << (BITS - 1)))
                dve.wait_ge(l_exp, 1)
                link(dve.tensor_reduce(g_top[:, :], G[:, :, :], AX, ALU.add))
                link(dve.reciprocal(g_top[:, :], g_top[:, :]))
                link(dve.tensor_tensor(G[:, :, :], G[:, :, :], one(g_top[:, :]), ALU.mult))

                def count(flags, n):
                    with nc.allow_low_precision(reason="sums up to 8 of zeros and ones"):
                        dve.tensor_reduce(flag_sum[:, :], flags.rearrange("p t e -> p e t"), AX, ALU.add)\
                            .then_inc(try_ready, 1)
                    dve.wait_ge(try_counted, n + 1)

                for n in range(BITS):
                    link(dve.tensor_tensor(flag[:, 0, :, :], G[:, :, :], every(try_cut[:, :]), ALU.is_ge))
                    count(flag[:, 0, :, :], n)
                    link(dve.scalar_tensor_tensor(try_ok[:, :], psM[:, n % 2, 0:E1], K1 - 0.5, try_cut[:, :],
                                                  ALU.is_gt, ALU.mult))
                    link(dve.tensor_tensor(low_cut[:, :], low_cut[:, :], try_ok[:, :], ALU.max))
                    if n < BITS - 1:
                        link(dve.tensor_scalar(try_cut[:, :].bitcast(I32), low_cut[:, :].bitcast(I32),
                                               1 << (BITS - 2 - n), None, ALU.bitwise_or))
                dve.tensor_tensor(equal[:, :, :], G[:, :, :], every(low_cut[:, :]), ALU.is_equal).then_inc(eq_ready, 1)
                link(dve.tensor_tensor(flag[:, 0, :, :], G[:, :, :], every(low_cut[:, :]), ALU.is_gt))
                count(flag[:, 0, :, :], BITS)
                link(dve.tensor_scalar(try_ok[:, :], psM[:, BITS % 2, 0:E1], -1.0, float(K1), ALU.mult, ALU.add))
                dve.wait_ge(eq_ranked, 1)
                link(dve.tensor_tensor(flag[:, 1, :, :], psX[:, 0, 0:NT * E1].rearrange("p (t e) -> p t e", t=NT),
                                       every(try_ok[:, :]), ALU.is_lt))
                link(dve.tensor_tensor(flag[:, 1, :, :], flag[:, 1, :, :], equal[:, :, :], ALU.mult))
                link(dve.tensor_tensor(flag[:, 0, :, :], flag[:, 0, :, :], flag[:, 1, :, :], ALU.add))
                dve.tensor_tensor(G[:, :, :], G[:, :, :], flag[:, 0, :, :], ALU.mult).then_inc(w_ready, 1)
                dve.wait_ge(w_ready, 1)
                for c in range(2):
                    dve.wait_ge(b2_done, c + 1)
                    dve.tensor_copy(Y[:, 4 * c:4 * c + 4, :], psM[:, c, :].rearrange("p (t d) -> p t d", t=4))\
                        .then_inc(b2_read, 1)
                dve.wait_ge(b2_read, 2)
                for u in range(2 * E1):
                    e, c = u // 2, u % 2
                    dve.wait_ge(d_down, u + 1)
                    if u >= 2:
                        dve.wait_ge(d_read, u - 1)
                    for t in range(4):
                        mm = dve.scalar_tensor_tensor(Y[:, 4 * c + t, :], psM[:, c, t * P:(t + 1) * P],
                                                      G[:, 4 * c + t, e:e + 1], Y[:, 4 * c + t, :], ALU.mult, ALU.add)
                    mm.then_inc(d_read, 1)
                dve.wait_ge(d_read, 2 * E1)
                link(dve.tensor_tensor(Y[:, :, :], Y[:, :, :], X[:, :, :], ALU.add))
                for b in range(B):
                    layer_norm(Y[:, QB * b:QB * (b + 1), :], X[:, QB * b:QB * (b + 1), :], b % 2).then_inc(final_ready, 1)

            def shared_h(c):
                dve.wait_ge(sh_silu, c + 1)
                dve.tensor_tensor(sh_hT[:, :, c * 512:(c + 1) * 512], silu_sh[:, c, :, :],
                                  psW[:, 1, :].rearrange("p (h n) -> p h n", h=2), ALU.mult).then_inc(sh_h, 1)

            dve.wait_ge(mask_loaded, 16)
            link(dve.memset(keys_row[:, :], 0.0))
            dve.tensor_scalar(keys_row[0:B, :], keys_i[:, :], 0.0, MASKED, ALU.is_equal, ALU.mult).then_inc(keys_made, 1)
            for buf in range(3):
                dve.memset(stackQ[64:ALL_ROWS, buf, :, :].rearrange("p h t -> p (h t)").bitcast(I32), ONES)\
                    .then_inc(q_rows_ready, 1)
            for lo, hi in SEGMENTS:
                for i in range(lo - 2, hi + 1):
                    early, mid, late, tail = i + 2 < hi, lo <= i + 1 < hi, lo <= i < hi, lo <= i - 1
                    chunk, n = 0, i + 2
                    for j in range(16):
                        if j == TURN_X and tail:
                            norm_outputs(i - 1, 1)
                        if j == PROJ_Q and early:
                            if n % B == 0:
                                dve.wait_ge(w_loaded[n // B], 16 * W_LOADS[n // B])
                            rest(n, q_hi, q_parts, q_rest, psB, bqk[:, n // B, 0:1], q_resid, q_split)
                        if j == PROJ_K and early:
                            rest(n, k_hi, k_parts, k_rest, psA, bqk[:, n // B, 1:2], k_resid, k_split)
                        if j == PROJ_V and early:
                            take_v(n)
                        if mid:
                            for _ in range(SCORES_IN_SLOT[j]):
                                row_max(i + 1, chunk)
                                chunk += 1
                                if chunk == 16:
                                    split_max(i + 1)
                        if j == PROJ_OUT and tail:
                            finish(i - 1)
                        if j == TURN_OUT and late:
                            norm_outputs(i, 0)
                    if i == -2:
                        dve.wait_ge(mask_loaded, 32)
                        dve.tensor_scalar(given[:, :, :], given_i[:, :, :], 0.0, MASKED, ALU.is_equal, ALU.mult)\
                            .then_inc(given_made, 1)
                        dve.memset(slot_rows[:, :, :, :], 0.0).then_inc(zero_ready, 1)
                if lo == 0:
                    feed_forward()
                    first_mixture()
                else:
                    second_mixture()

        @block.gpsimd
        def _(pool):
            chain = [0]

            def link(ins):
                chain[0] += 1
                ins.then_inc(pool_chain, 1)
                pool.wait_ge(pool_chain, chain[0])

            pool.dma_start(keys_i[:, :], a["mask_Bx1x1xS2_if1"].rearrange("b x y k -> b (x y k)")).then_inc(mask_loaded, 16)
            for t in (ident, ident_b):
                link(pool.memset(t[:, :], 0.0))
                link(pool.affine_select(out=t[:, :], in_=t[:, :], compare_op=ALU.not_equal, fill=1.0, base=0,
                                        pattern=[[-1, P]], channel_multiplier=1))
            link(pool.memset(tri[:, :, :], 0.0))
            link(pool.affine_select(out=tri[:, 0, :], in_=tri[:, 0, :], compare_op=ALU.is_ge, fill=MASKED, base=0,
                                    pattern=[[-1, P]], channel_multiplier=1))
            pool.affine_select(out=tri[:, 1, :], in_=tri[:, 1, :], compare_op=ALU.is_ge, fill=MASKED, base=0,
                               pattern=[[1, P]], channel_multiplier=-1).then_inc(const_ready, 1)
            pool.wait_ge(const_ready, 1)
            for buf in range(3):
                pool.memset(stackK[64:ALL_ROWS, buf, :, :].rearrange("p h t -> p (h t)").bitcast(I32), ONES)\
                    .then_inc(k_rows_ready, 1)
                pool.wait_ge(k_rows_ready, buf + 1)
                link(pool.memset(v_aug[:, buf, :, :, DH:32], 0.0))
                pool.memset(v_aug[:, buf, :, :, DH:DH + 1], 1.0).then_inc(v_const, 1)
                pool.wait_ge(v_const, buf + 1)
            pool.wait_ge(mask_loaded, 16)
            pool.dma_start(given_i[:, :, :], a["mask_1x1xSxS2_ik0"].rearrange("a c (t p) k -> p (a c t) k", p=P))\
                .then_inc(mask_loaded, 16)
            link(pool.memset(neg_half[:, :], -0.5))

            def make_others():
                link(pool.memset(ones_b[:, :], 1.0))
                link(pool.affine_select(out=before_b[:, :], in_=ones_b[:, :], compare_op=ALU.is_gt, fill=0.0, base=0,
                                        pattern=[[1, P]], channel_multiplier=-1))
                link(pool.memset(lower[:, :, :], 1.0))
                link(pool.affine_select(out=lower[:, :, :], in_=lower[:, :, :], compare_op=ALU.is_gt, fill=0.0, base=0,
                                        pattern=[[1, G0], [-1, G0]], channel_multiplier=0))
                pool.iota(iota_e[:, :], pattern=[[1, E0]], base=0, channel_multiplier=0,
                          allow_small_or_imprecise_dtypes=True).then_inc(mix_const, 1)

            def low_part(n, mid, restof, parts, ready):
                pool.wait_ge(mid, n + 1)
                pool.tensor_tensor(parts[:, n % 2, 2, :], restof[:, n % 2, :], parts[:, n % 2, 1, :],
                                   ALU.subtract).then_inc(ready, 1)

            def root(par):
                norms[0] += 1
                pool.wait_ge(var_ready, norms[0])
                pool.tensor_tensor(rstd[:, par, :], var_eps[:, par, :], neg_half[:, 0:QB], ALU.pow).then_inc(rstd_ready, 1)

            def first_mixture():
                pool.wait_ge(pow_in, 1)
                pool.tensor_tensor(cent_n[:, 1:2], cent_n[:, 0:1], neg_half[0:G0 + E0, 0:1], ALU.pow).then_inc(pow_out, 1)
                pool.wait_ge(pow_in, 2)
                pool.tensor_tensor(norm_x[:, 1, :], norm_x[:, 0, :], neg_half[:, :], ALU.pow).then_inc(pow_out, 1)
                pool.wait_ge(slots_ready, 1)
                pool.wait_ge(zero_stored, 16 * (ST // 8))
                for t in range(NT):
                    for k in range(K0):
                        j = t * K0 + k
                        pool.indirect_dma_start(
                            out=slot_x_dram, out_offset=bass.IndirectOffsetOnAxis(ap=slot_to[:, j:j + 1], axis=0),
                            in_=X[:, t, :], in_offset=None, bounds_check=SLOTS - 1, oob_is_err=False)\
                            .then_inc(scattered, 16)
                for j in range(2):
                    pool.wait_ge(y_stored[j], 16 * (E0 // 2))
                pool.wait_ge(e_up, E0)
                for t in range(NT):
                    for k in range(K0):
                        j = t * K0 + k
                        pool.indirect_dma_start(
                            out=y_chosen[:, j, :], out_offset=None, in_=slot_y_dram,
                            in_offset=bass.IndirectOffsetOnAxis(ap=slot_from[:, j:j + 1], axis=0),
                            bounds_check=SLOTS - 1, oob_is_err=False).then_inc(gathered[t], 16)
                for b in range(B):
                    root(b % 2)

            norms = [0]
            for lo, hi in SEGMENTS:
                for i in range(lo - 2, hi + 1):
                    if i + 2 < hi:
                        low_part(i + 2, q_mid, q_rest, q_parts, q_split)
                        low_part(i + 2, k_mid, k_rest, k_parts, k_split)
                    if i == 0:
                        make_others()
                    if lo <= i - 1:
                        root((i - 1) % 2)
                if lo == 0:
                    for b in range(B):
                        root(b % 2)
                        root(b % 2)
                    first_mixture()
                if lo > 0:
                    for b in range(B):
                        root(b % 2)


BY_HEAD = ["L0_attn_Wq", "L0_attn_Wk", "L0_xattn_s_wq", "L0_xattn_s_wk", "L0_xattn_c_wq", "L0_xattn_c_wk",
           "L0_xattn_s_bq", "L0_xattn_s_bk", "L0_xattn_c_bq", "L0_xattn_c_bk", "L1_xattn_bq", "L1_xattn_bk"]


def by_dimension(name, v):
    if name in BY_HEAD:
        return v.reshape(v.shape[:-1] + (NH, DH)).swapaxes(-1, -2).reshape(v.shape)
    if name in ("L1_xattn_Wq", "L1_xattn_Wk"):
        return v.reshape(NH, DH, D).swapaxes(0, 1).reshape(D, D)
    if name in ("L1_attn_w_in", "L1_attn_b_in"):
        v = v.copy()
        for c in range(2):
            part = v[c * D:(c + 1) * D]
            v[c * D:(c + 1) * D] = part.reshape((NH, DH) + part.shape[1:]).swapaxes(0, 1).reshape(part.shape)
    return v


def kernel(**inputs):
    import numpy as _np
    import concourse.bacc as _bacc
    from concourse import mybir as _mybir
    from concourse.bass_utils import run_bass_kernel_spmd as _run

    nc = _bacc.Bacc("TRN2", target_bir_lowering=False, num_devices=1)
    arrays, args = {}, {}
    for name, value in inputs.items():
        v = _np.ascontiguousarray(by_dimension(name, _np.asarray(value)))
        arrays[f"in_{name}"] = v
        args[name] = nc.dram_tensor(f"in_{name}", v.shape, _mybir.dt.from_np(v.dtype), kind="ExternalInput").ap()
    out = nc.dram_tensor("out", (B, S, D), F32, kind="ExternalOutput").ap()
    build(nc, args, out)
    r = _run(nc, [arrays], core_ids=[0])
    return r.results[0]["out"]
```
